# Optimizing a Trainium2 kernel written in Bass

```python
import numpy as np
import jax
import jax.numpy as jnp

def _softmax(x, axis=-1):
    return jax.nn.softmax(x, axis=axis)

def _gelu(x):
    return jax.nn.gelu(x, approximate=True)

def _silu(x):
    return jax.nn.silu(x)

def _sigmoid(x):
    return jax.nn.sigmoid(x)

def _layernorm(x, axis=-1, eps=1e-05):
    m = jnp.mean(x, axis=axis, keepdims=True)
    v = jnp.var(x, axis=axis, keepdims=True)
    return (x - m) / jnp.sqrt(v + eps)

def _scatter_add(tgt, idx, src, axis=0):
    return tgt.at[idx].add(src)

def _segment_sum(src, seg, n):
    return jax.ops.segment_sum(src, seg, n)
kernel_name = 'mk_lm_tower_d1_tok_ids512_r4_80dfd7'

def setup_inputs(seed: int=0):
    np.random.seed(seed)
    _w = jnp.asarray

    def _rec_inputs():
        import jax
        import jax.numpy as jnp
        _rk = jax.random.key(seed)
        x = jax.random.randint(jax.random.fold_in(_rk, 1), (8, 2048), 0, 1250, jnp.int32)
        return x
    x = _rec_inputs()

    def _L0_tok_setup():
        import jax, jax.numpy as jnp
        import numpy as np
        import math
        D_MODEL = 128
        MAX_LEN = 1250

        def _make_pe(max_len=MAX_LEN, d_model=D_MODEL):
            position = np.arange(max_len, dtype=np.float32)[:, None]
            div_term = np.exp(np.arange(0, d_model, 2, dtype=np.float32) * -(math.log(10000.0) / d_model))
            pe = np.zeros((max_len, d_model), dtype=np.float32)
            pe[:, 0::2] = np.sin(position * div_term)
            pe[:, 1::2] = np.cos(position * div_term)
            return jnp.asarray(pe)
        key = jax.random.key(seed)
        k1, _ = jax.random.split(key)
        delta_t = jax.random.randint(k1, (64, 1024), 0, MAX_LEN, dtype=jnp.int64 if jax.config.read('jax_enable_x64') else jnp.int32)
        pe = _make_pe()
        return {'delta_t': delta_t, 'pe': pe}
    _L0_tok_all = _L0_tok_setup()
    _L0_tok_in = {k: v for k, v in _L0_tok_all.items() if k in ('pe',)}
    del _L0_tok_all

    def _L0_attn_setup():
        import jax, jax.numpy as jnp
        import numpy as np
        from jax import lax
        B, S, D = (2, 2048, 128)
        INNER, NH, KCONV, L = (256, 8, 4, 64)
        DH = INNER // NH
        EPS = 1e-06

        def _mlstm_chunkwise(q, k, v, vecI, vecF, chunk, qk_scale, eps):
            b, nh, s, dh = q.shape
            nc = s // chunk
            qc = q.reshape(b, nh, nc, chunk, dh)
            kc = k.reshape(b, nh, nc, chunk, dh)
            vc = v.reshape(b, nh, nc, chunk, dh)
            Ic = vecI.reshape(b, nh, nc, chunk)
            Fc = vecF.reshape(b, nh, nc, chunk)
            vecB = jnp.cumsum(Fc, axis=-1)
            scaG = vecB[..., -1]
            vecA = scaG[..., None] - vecB + Ic
            k_sc = jnp.moveaxis(kc, 2, 0)
            v_sc = jnp.moveaxis(vc, 2, 0)
            g_sc = jnp.moveaxis(scaG, 2, 0)
            a_sc = jnp.moveaxis(vecA, 2, 0)
            C0 = jnp.zeros((b, nh, dh, dh), q.dtype)
            n0 = jnp.zeros((b, nh, dh), q.dtype)
            m0 = jnp.zeros((b, nh), q.dtype)

            def step(carry, inp):
                C, n, m = carry
                kk, vv, g, a = inp
                m_new = jnp.maximum(g + m, a.max(-1))
                kbar = kk * jnp.exp(a - m_new[..., None])[..., None]
                dec = jnp.exp(g + m - m_new)
                C_new = dec[..., None, None] * C + jnp.einsum('bhld,bhle->bhde', kbar, vv)
                n_new = dec[..., None] * n + kbar.sum(-2)
                return ((C_new, n_new, m_new), (C, n, m))
            _, (Cs, ns, ms) = lax.scan(step, (C0, n0, m0), (k_sc, v_sc, g_sc, a_sc))
            Cs = jnp.moveaxis(Cs, 0, 2)
            ns = jnp.moveaxis(ns, 0, 2)
            ms = jnp.moveaxis(ms, 0, 2)
            logD = vecB[..., :, None] - vecB[..., None, :] + Ic[..., None, :]
            mask = jnp.tril(jnp.ones((chunk, chunk), bool))
            logD = jnp.where(mask, logD, -jnp.inf)
            m_intra = logD.max(-1)
            m_comb = jnp.maximum(vecB + ms[..., None], m_intra)
            Dmat = jnp.exp(logD - m_comb[..., None])
            Smat = jnp.einsum('bhcid,bhcjd->bhcij', qc, kc) * qk_scale * Dmat
            qbar = qc * qk_scale * jnp.exp(vecB + ms[..., None] - m_comb)[..., None]
            num = jnp.einsum('bhcld,bhcde->bhcle', qbar, Cs) + jnp.einsum('bhcij,bhcje->bhcie', Smat, vc)
            den_l = jnp.einsum('bhcld,bhcd->bhcl', qbar, ns) + Smat.sum(-1)
            den = jnp.maximum(jnp.abs(den_l), jnp.exp(-m_comb)) + eps
            h = num / den[..., None]
            return h.reshape(b, nh, s, dh)

        def _forward(x, W_up, Wq, Wk, Wv, W_ig, b_ig, W_fg, b_fg, conv_w, conv_b, skip, W_down):
            b, s, d = x.shape
            x_up = x @ W_up.T
            x_mlstm, x_og = jnp.split(x_up, 2, axis=-1)
            xc = x_mlstm.transpose(0, 2, 1)
            kern = conv_w[:, None, :]
            y = lax.conv_general_dilated(xc, kern, (1,), [(KCONV - 1, 0)], dimension_numbers=('NCH', 'OIH', 'NCH'), feature_group_count=INNER)
            x_mlstm = jax.nn.silu((y + conv_b[None, :, None]).transpose(0, 2, 1))
            q = (x_mlstm @ Wq.T).reshape(b, s, NH, DH).transpose(0, 2, 1, 3)
            k = (x_mlstm @ Wk.T).reshape(b, s, NH, DH).transpose(0, 2, 1, 3)
            v = (x_mlstm @ Wv.T).reshape(b, s, NH, DH).transpose(0, 2, 1, 3)
            i_pre = (x_mlstm @ W_ig.T + b_ig).transpose(0, 2, 1)
            f_pre = (x_mlstm @ W_fg.T + b_fg).transpose(0, 2, 1)
            vecI = jnp.log(jax.nn.sigmoid(i_pre) + EPS)
            vecF = jnp.log(jax.nn.sigmoid(f_pre) + EPS)
            h = _mlstm_chunkwise(q, k, v, vecI, vecF, L, DH ** (-0.5), EPS)
            h = h.transpose(0, 2, 1, 3).reshape(b, s, INNER)
            h = h + skip * x_mlstm
            h = h * jax.nn.silu(x_og)
            return h @ W_down.T
        key = jax.random.key(seed)
        ks = jax.random.split(key, 12)
        sc = 0.02
        return {'x': jax.random.normal(ks[0], (B, S, D), jnp.float32), 'W_up': jax.random.normal(ks[1], (2 * INNER, D), jnp.float32) * sc, 'Wq': jax.random.normal(ks[2], (INNER, INNER), jnp.float32) * sc, 'Wk': jax.random.normal(ks[3], (INNER, INNER), jnp.float32) * sc, 'Wv': jax.random.normal(ks[4], (INNER, INNER), jnp.float32) * sc, 'W_ig': jax.random.normal(ks[5], (NH, INNER), jnp.float32) * sc, 'b_ig': jnp.zeros((NH,), jnp.float32), 'W_fg': jax.random.normal(ks[6], (NH, INNER), jnp.float32) * sc, 'b_fg': jnp.linspace(3.0, 6.0, NH, dtype=jnp.float32), 'conv_w': jax.random.normal(ks[7], (INNER, KCONV), jnp.float32) * sc, 'conv_b': jnp.zeros((INNER,), jnp.float32), 'skip': jnp.ones((INNER,), jnp.float32), 'W_down': jax.random.normal(ks[8], (D, INNER), jnp.float32) * sc}
    _L0_attn_all = _L0_attn_setup()
    _L0_attn_in = {k: v for k, v in _L0_attn_all.items() if k in ('W_up', 'Wq', 'Wk', 'Wv', 'W_ig', 'b_ig', 'W_fg', 'b_fg', 'conv_w', 'conv_b', 'skip', 'W_down')}
    del _L0_attn_all

    def _L0_ffn_setup():
        import jax, jax.numpy as jnp
        import numpy as np
        B, S, D, H, E = (4, 512, 128, 256, 8)
        key = jax.random.key(seed)
        ks = jax.random.split(key, 4)
        x = jax.random.normal(ks[0], (B, S, D), jnp.float32)
        Wr = jax.random.normal(ks[1], (E, D), jnp.float32) * 0.02
        br = jnp.zeros((E,), jnp.float32)
        W1 = jax.random.normal(ks[2], (E, D, H), jnp.float32) * 0.02
        b1 = jnp.zeros((E, H), jnp.float32)
        W2 = jax.random.normal(ks[3], (E, H, D), jnp.float32) * 0.02
        b2 = jnp.zeros((E, D), jnp.float32)
        return {'x': x, 'Wr': Wr, 'br': br, 'W1': W1, 'b1': b1, 'W2': W2, 'b2': b2}
    _L0_ffn_all = _L0_ffn_setup()
    _L0_ffn_in = {k: v for k, v in _L0_ffn_all.items() if k in ('Wr', 'br', 'W1', 'b1', 'W2', 'b2')}
    del _L0_ffn_all
    return {'x': x, 'L0_tok_pe': _L0_tok_in['pe'], 'L0_attn_W_up': _L0_attn_in['W_up'], 'L0_attn_Wq': _L0_attn_in['Wq'], 'L0_attn_Wk': _L0_attn_in['Wk'], 'L0_attn_Wv': _L0_attn_in['Wv'], 'L0_attn_W_ig': _L0_attn_in['W_ig'], 'L0_attn_b_ig': _L0_attn_in['b_ig'], 'L0_attn_W_fg': _L0_attn_in['W_fg'], 'L0_attn_b_fg': _L0_attn_in['b_fg'], 'L0_attn_conv_w': _L0_attn_in['conv_w'], 'L0_attn_conv_b': _L0_attn_in['conv_b'], 'L0_attn_skip': _L0_attn_in['skip'], 'L0_attn_W_down': _L0_attn_in['W_down'], 'L0_ffn_Wr': _L0_ffn_in['Wr'], 'L0_ffn_br': _L0_ffn_in['br'], 'L0_ffn_W1': _L0_ffn_in['W1'], 'L0_ffn_b1': _L0_ffn_in['b1'], 'L0_ffn_W2': _L0_ffn_in['W2'], 'L0_ffn_b2': _L0_ffn_in['b2']}

def reference(x, L0_tok_pe, L0_attn_W_up, L0_attn_Wq, L0_attn_Wk, L0_attn_Wv, L0_attn_W_ig, L0_attn_b_ig, L0_attn_W_fg, L0_attn_b_fg, L0_attn_conv_w, L0_attn_conv_b, L0_attn_skip, L0_attn_W_down, L0_ffn_Wr, L0_ffn_br, L0_ffn_W1, L0_ffn_b1, L0_ffn_W2, L0_ffn_b2):
    import jax
    import jax.numpy as jnp

    def _L0_tok_ref(delta_t, pe):
        import jax, jax.numpy as jnp
        import numpy as np
        import math
        D_MODEL = 128
        MAX_LEN = 1250

        def _make_pe(max_len=MAX_LEN, d_model=D_MODEL):
            position = np.arange(max_len, dtype=np.float32)[:, None]
            div_term = np.exp(np.arange(0, d_model, 2, dtype=np.float32) * -(math.log(10000.0) / d_model))
            pe = np.zeros((max_len, d_model), dtype=np.float32)
            pe[:, 0::2] = np.sin(position * div_term)
            pe[:, 1::2] = np.cos(position * div_term)
            return jnp.asarray(pe)
        return pe[delta_t]

    def _L0_attn_ref(x, W_up, Wq, Wk, Wv, W_ig, b_ig, W_fg, b_fg, conv_w, conv_b, skip, W_down):
        import jax, jax.numpy as jnp
        import numpy as np
        from jax import lax
        B, S, D = (2, 2048, 128)
        INNER, NH, KCONV, L = (256, 8, 4, 64)
        DH = INNER // NH
        EPS = 1e-06

        def _mlstm_chunkwise(q, k, v, vecI, vecF, chunk, qk_scale, eps):
            b, nh, s, dh = q.shape
            nc = s // chunk
            qc = q.reshape(b, nh, nc, chunk, dh)
            kc = k.reshape(b, nh, nc, chunk, dh)
            vc = v.reshape(b, nh, nc, chunk, dh)
            Ic = vecI.reshape(b, nh, nc, chunk)
            Fc = vecF.reshape(b, nh, nc, chunk)
            vecB = jnp.cumsum(Fc, axis=-1)
            scaG = vecB[..., -1]
            vecA = scaG[..., None] - vecB + Ic
            k_sc = jnp.moveaxis(kc, 2, 0)
            v_sc = jnp.moveaxis(vc, 2, 0)
            g_sc = jnp.moveaxis(scaG, 2, 0)
            a_sc = jnp.moveaxis(vecA, 2, 0)
            C0 = jnp.zeros((b, nh, dh, dh), q.dtype)
            n0 = jnp.zeros((b, nh, dh), q.dtype)
            m0 = jnp.zeros((b, nh), q.dtype)

            def step(carry, inp):
                C, n, m = carry
                kk, vv, g, a = inp
                m_new = jnp.maximum(g + m, a.max(-1))
                kbar = kk * jnp.exp(a - m_new[..., None])[..., None]
                dec = jnp.exp(g + m - m_new)
                C_new = dec[..., None, None] * C + jnp.einsum('bhld,bhle->bhde', kbar, vv)
                n_new = dec[..., None] * n + kbar.sum(-2)
                return ((C_new, n_new, m_new), (C, n, m))
            _, (Cs, ns, ms) = lax.scan(step, (C0, n0, m0), (k_sc, v_sc, g_sc, a_sc))
            Cs = jnp.moveaxis(Cs, 0, 2)
            ns = jnp.moveaxis(ns, 0, 2)
            ms = jnp.moveaxis(ms, 0, 2)
            logD = vecB[..., :, None] - vecB[..., None, :] + Ic[..., None, :]
            mask = jnp.tril(jnp.ones((chunk, chunk), bool))
            logD = jnp.where(mask, logD, -jnp.inf)
            m_intra = logD.max(-1)
            m_comb = jnp.maximum(vecB + ms[..., None], m_intra)
            Dmat = jnp.exp(logD - m_comb[..., None])
            Smat = jnp.einsum('bhcid,bhcjd->bhcij', qc, kc) * qk_scale * Dmat
            qbar = qc * qk_scale * jnp.exp(vecB + ms[..., None] - m_comb)[..., None]
            num = jnp.einsum('bhcld,bhcde->bhcle', qbar, Cs) + jnp.einsum('bhcij,bhcje->bhcie', Smat, vc)
            den_l = jnp.einsum('bhcld,bhcd->bhcl', qbar, ns) + Smat.sum(-1)
            den = jnp.maximum(jnp.abs(den_l), jnp.exp(-m_comb)) + eps
            h = num / den[..., None]
            return h.reshape(b, nh, s, dh)

        def _forward(x, W_up, Wq, Wk, Wv, W_ig, b_ig, W_fg, b_fg, conv_w, conv_b, skip, W_down):
            b, s, d = x.shape
            x_up = x @ W_up.T
            x_mlstm, x_og = jnp.split(x_up, 2, axis=-1)
            xc = x_mlstm.transpose(0, 2, 1)
            kern = conv_w[:, None, :]
            y = lax.conv_general_dilated(xc, kern, (1,), [(KCONV - 1, 0)], dimension_numbers=('NCH', 'OIH', 'NCH'), feature_group_count=INNER)
            x_mlstm = jax.nn.silu((y + conv_b[None, :, None]).transpose(0, 2, 1))
            q = (x_mlstm @ Wq.T).reshape(b, s, NH, DH).transpose(0, 2, 1, 3)
            k = (x_mlstm @ Wk.T).reshape(b, s, NH, DH).transpose(0, 2, 1, 3)
            v = (x_mlstm @ Wv.T).reshape(b, s, NH, DH).transpose(0, 2, 1, 3)
            i_pre = (x_mlstm @ W_ig.T + b_ig).transpose(0, 2, 1)
            f_pre = (x_mlstm @ W_fg.T + b_fg).transpose(0, 2, 1)
            vecI = jnp.log(jax.nn.sigmoid(i_pre) + EPS)
            vecF = jnp.log(jax.nn.sigmoid(f_pre) + EPS)
            h = _mlstm_chunkwise(q, k, v, vecI, vecF, L, DH ** (-0.5), EPS)
            h = h.transpose(0, 2, 1, 3).reshape(b, s, INNER)
            h = h + skip * x_mlstm
            h = h * jax.nn.silu(x_og)
            return h @ W_down.T
        return _forward(x, W_up, Wq, Wk, Wv, W_ig, b_ig, W_fg, b_fg, conv_w, conv_b, skip, W_down)

    def _L0_ffn_ref(x, Wr, br, W1, b1, W2, b2):
        import jax, jax.numpy as jnp
        import numpy as np
        B, S, D, H, E = (4, 512, 128, 256, 8)
        b, s, d = x.shape
        n = b * s
        e = Wr.shape[0]
        xf = x.reshape(n, d)
        logits = xf @ Wr.T + br
        probs = jax.nn.softmax(logits, axis=-1)
        top2_prob, top2_idx = jax.lax.top_k(probs, 2)
        comb = jnp.zeros((n, e), x.dtype).at[jnp.arange(n)[:, None], top2_idx].add(top2_prob)
        h = jax.nn.gelu(jnp.einsum('nd,edh->enh', xf, W1) + b1[:, None, :], approximate=False)
        o = jnp.einsum('enh,ehd->end', h, W2) + b2[:, None, :]
        y = jnp.einsum('ne,end->nd', comb, o)
        return y.reshape(b, s, d)
    h = _L0_tok_ref(x, L0_tok_pe)
    h = h + _L0_attn_ref(_layernorm(h, axis=-1), L0_attn_W_up, L0_attn_Wq, L0_attn_Wk, L0_attn_Wv, L0_attn_W_ig, L0_attn_b_ig, L0_attn_W_fg, L0_attn_b_fg, L0_attn_conv_w, L0_attn_conv_b, L0_attn_skip, L0_attn_W_down)
    h = h + _L0_ffn_ref(_layernorm(h, axis=-1), L0_ffn_Wr, L0_ffn_br, L0_ffn_W1, L0_ffn_b1, L0_ffn_W2, L0_ffn_b2)
    return h

_drawn_inputs = setup_inputs


def setup_inputs(seed=0):
    import zlib

    import numpy as np

    out = dict(_drawn_inputs(seed))
    spreads = {'L0_attn_b_ig': (0.0, 0.8),
     'L0_attn_conv_b': (0.0, 0.8),
     'L0_attn_skip': (1.0, 0.6),
     'L0_ffn_br': (0.0, 0.296),
     'L0_ffn_b1': (0.0, 2.0),
     'L0_ffn_b2': (0.0, 0.8)}
    factors = {'L0_attn_W_up': 8.0,
     'L0_attn_Wq': 8.0,
     'L0_attn_Wk': 8.0,
     'L0_attn_Wv': 8.0,
     'L0_attn_W_ig': 8.0,
     'L0_attn_W_fg': 8.0,
     'L0_attn_b_fg': 8.0,
     'L0_attn_conv_w': 8.0,
     'L0_attn_W_down': 8.0,
     'L0_ffn_W1': 4.296,
     'L0_ffn_W2': 4.065,
     'L0_ffn_Wr': 2.889}
    for name, (base, spread) in spreads.items():
        noise = np.random.default_rng([zlib.crc32(name.encode()), seed]).standard_normal(out[name].shape)
        drawn = base * np.exp(spread * noise) if base else spread * noise
        out[name] = jnp.asarray(drawn.astype(out[name].dtype))
    for name, factor in factors.items():
        out[name] = (out[name] * factor).astype(out[name].dtype)
    return out
```

```python
from contextlib import ExitStack

import concourse.bass as bass
from concourse import mybir

F32 = mybir.dt.float32
I32 = mybir.dt.int32
ALU = mybir.AluOpType
ACT = mybir.ActivationFunctionType

P = 128
LN_EPS = 1e-5
GATE_EPS = 1e-6
MASKED = -1e30


class Step:

    def __init__(self, chunk, group):
        self.c, self.g = chunk, group
        self.n = 2 * chunk + group
        self.exists = not (isinstance(chunk, int) and chunk < 0)

    @property
    def prev(self):
        return Step(self.c, 0) if self.g else Step(self.c - 1, 1)

    @property
    def next(self):
        return Step(self.c + 1, 0) if self.g else Step(self.c, 1)

    @property
    def before(self):
        return Step(self.c - 1, self.g)

    @property
    def after(self):
        return Step(self.c + 1, self.g)


def wait(engine, sem, per_step, step, i):
    if step.exists:
        engine.wait_ge(sem, per_step * step.n + i)


def wait_dma(engine, sems, step, dmas=1):
    if step.exists:
        engine.wait_ge(sems[step.g], 16 * dmas * (step.c + 1))


def wait_apart(engine, done, *waits):
    values = [v if isinstance(v, int) else engine.lower_val(v) for _, v in waits]
    engine.wait_ge(*done)
    for (sem, _), v in zip(waits, values):
        engine.wait_ge(sem, v)


def build(nc, x, pe, w_up, w_q, w_k, w_v, w_ig, b_ig, w_fg, b_fg, conv_w, conv_b, skip, w_down, w_r, b_r, w1, b1, w2, b2, out):
    B, S = x.shape
    VOCAB, D = pe.shape
    INNER = w_q.shape[0]
    NH = w_ig.shape[1]
    TAPS = conv_w.shape[1]
    DH = INNER // NH
    L = P
    NC = S // L
    G = B // 2
    KT = INNER // P
    HPK = NH // KT
    E1 = DH + 1
    GH = G * NH
    RW = L + 1
    VT = 10
    VR = VOCAB // VT
    PO = D + INNER
    GT = G * L
    assert VR * VT == VOCAB and KT == 2 and HPK == 4 and D == P and GT == 512 and NC * B == P

    NE, _, FH = w1.shape
    FK = FH // P
    TOP = 2
    TR = 4 * P
    RPT = TR // P
    REGION = B * S + TR
    MIN_TILES = TOP * B * S // TR
    NT = MIN_TILES + NE
    SLOT_ROWS = NE * REGION + NE * TR
    NSTEP = 2 * NC
    TILE_SHIFT = TR.bit_length() - 1
    assert FK == 2 and NT % 2 == 0 and TR == 1 << TILE_SHIFT and SLOT_ROWS < 1 << 24

    h1 = nc.dram_tensor("h1", (B, S, D), F32, kind="Internal").ap()
    slot_in = nc.dram_tensor("slot_in", (SLOT_ROWS, D), F32, kind="Internal").ap()
    slot_out = nc.dram_tensor("slot_out", (NT * TR, D), F32, kind="Internal").ap()
    table_x = nc.dram_tensor("table_x", (VOCAB, INNER), F32, kind="Internal").ap()
    table_po = nc.dram_tensor("table_po", (VOCAB, PO), F32, kind="Internal").ap()
    stab_dram = nc.dram_tensor("stab_dram", (2, GH * RW), F32, kind="Internal").ap()

    with ExitStack() as ctx:
        def sb(name, shape, dt=F32):
            return ctx.enter_context(nc.sbuf_tensor(name, shape, dt))

        def sem(name):
            return ctx.enter_context(nc.semaphore(name))

        def sem2(name):
            return [sem(f"{name}{g}") for g in range(2)]

        bank = [ctx.enter_context(nc.psum_tensor(f"bank{i}", [P, 512], F32)) for i in range(8)]
        SC, PJ, OX = bank[0:4], bank[4:6], bank[6:8]

        wr = sb("wr", [P, NE])
        brb = sb("brb", [P, NE])
        expert_i = sb("expert_i", [P, NE], I32)
        expert_f = sb("expert_f", [P, NE])
        region_i = sb("region_i", [P, NE], I32)
        region_f = sb("region_f", [P, NE])
        tile_i = sb("tile_i", [1, NT], I32)
        tile_f = sb("tile_f", [1, NT])
        earlier = sb("earlier", [P, P])
        ones_pp = sb("ones_pp", [P, P])
        zero_rows = sb("zero_rows", [P, D])
        total = sb("total", [P, NE])
        total_up = sb("total_up", [P, NE], I32)
        b1_stage = sb("b1_stage", [P, FK, NE])
        tiles_i = sb("tiles_i", [P, NE], I32)
        tiles_f = sb("tiles_f", [P, NE])
        shift = sb("shift", [P, NE])
        tiles_end = sb("tiles_end", [1, NE])
        ones_e = sb("ones_e", [1, NE])
        pad_row = sb("pad_row", [1, NE], I32)
        tile_expert = sb("tile_expert", [1, NT])
        tile_start = sb("tile_start", [1, NT])
        tile_in = sb("tile_in", [1, NT])
        tile_base = sb("tile_base", [1, NT])
        w1_all = sb("w1_all", [P, NE, FH + FK])
        w2_all = sb("w2_all", [P, NE, (FK + 1) * D])
        tally = sb("tally", [P, G, NE])
        slots_all = sb("slots_all", [P, NSTEP, TOP * G])
        out_slots = sb("out_slots", [P, NSTEP, TOP * G], I32)
        probs_all = sb("probs_all", [P, NSTEP, TOP * G])
        row_of = sb("row_of", [1, NT], I32)
        expert_of = sb("expert_of", [1, NT], I32)
        ident = sb("ident", [P, P])

        with ExitStack() as early_ctx:
            def early(name, shape, dt=F32):
                return early_ctx.enter_context(nc.sbuf_tensor(name, shape, dt))

            wup = early("wup", [P, 2 * INNER])
            pe_sb = early("pe_sb", [VR, VT, D])
            stats = early("stats", [VR, VT, 6])
            moments = early("moments", [VR, VT, 2])
            spread = early("spread", [VR, VT])
            rstd = early("rstd", [VR, VT])
            emb_n = early("emb_n", [VR, VT, D])
            emb_nT = early("emb_nT", [P, 2, VR])
            tx_sb = early("tx_sb", [VR, VT, INNER])
            tpo_sb = early("tpo_sb", [VR, VT, PO])
            ids_i = early("ids_i", [P, L], I32)
            ids_f = early("ids_f", [P, L])
        with ExitStack() as mixer_ctx:
            def mix(name, shape, dt=F32):
                return mixer_ctx.enter_context(nc.sbuf_tensor(name, shape, dt))

            decay = [mix(f"decay{g}", [P, GH, RW]) for g in range(2)]
            y = mix("y", [P, KT, GT])
            y_s = mix("y_s", [P, KT, GT])

            wq = mix("wq", [P, KT, INNER])
            wk = mix("wk", [P, KT, INNER])
            wvg = mix("wvg", [P, KT, INNER + 2 * NH])
            wd = mix("wd", [P, KT, D])
            taps = mix("taps", [P, KT, TAPS])
            convb = mix("convb", [P, KT])
            skipc = mix("skipc", [P, KT])
            gbias = mix("gbias", [P, G, 2, NH])
            ones_row = mix("ones_row", [GH, L])

            ids_T = mix("ids_T", [P, NC + 1, B], I32)

            x_idx = [mix(f"x_idx{g}", [P, G], I32) for g in range(2)]
            po_idx = [mix(f"po_idx{g}", [P, G], I32) for g in range(2)]
            x_rows = [mix(f"x_rows{g}", [P, G, INNER]) for g in range(2)]
            po_rows = [mix(f"po_rows{g}", [P, G, PO]) for g in range(2)]
            xup = [mix(f"xup{g}", [P, KT, G, TAPS - 1 + L]) for g in range(2)]
            conv = mix("conv", [P, KT, G, L])
            xm = [mix(f"xm{g}", [P, KT, GT]) for g in range(2)]
            qT = mix("qT", [P, KT, GT])
            kT = mix("kT", [P, KT, GT])
            k_tm = mix("k_tm", [P, G, INNER])
            v1 = [mix(f"v1{g}", [P, G, KT, HPK, HPK, E1]) for g in range(2)]
            v_w = mix("v_w", [P, GH, E1])
            gates = mix("gates", [P, G, 2, NH])
            gate_e = mix("gate_e", [P, G, 2, NH])
            gate_d = mix("gate_d", [P, G, 2, NH])
            gate_r = mix("gate_r", [P, G, 2, NH])
            gate_s = mix("gate_s", [P, G, 2, NH])
            gate_log = mix("gate_log", [P, 2, GH])
            rows_if = mix("rows_if", [GH, 2, L])
            row_b = mix("row_b", [GH, L])
            row_m = mix("row_m", [GH, L])
            m_carry = [mix(f"m_carry{g}", [GH, 1]) for g in range(2)]
            row_f = mix("row_f", [GH, 4, L])
            row_stab = mix("row_stab", [GH, RW])
            cols = [mix(f"cols{g}", [P, 4, GH]) for g in range(2)]
            state = [mix(f"state{g}", [P, G, NH, E1]) for g in range(2)]
            state_d = mix("state_d", [P, G, NH, E1])
            inter = mix("inter", [P, NH, E1])
            osum = mix("osum", [P, G, NH, E1])
            den = mix("den", [P, 4, GH])
            h_tm = mix("h_tm", [P, G, INNER])
            h1_sb = [mix(f"h1_sb{g}", [P, G, D]) for g in range(2)]
            ln_stats = mix("ln_stats", [P, G, 6])
            ln_mv = mix("ln_mv", [P, G, 2])
            ln_var = mix("ln_var", [P, G])
            minus_half = mix("minus_half", [P, G])
            ln_rstd = mix("ln_rstd", [P, G])
            xn = [mix(f"xn{g}", [P, G, D]) for g in range(2)]
            xnT = mix("xnT", [P, GT])
            logits = mix("logits", [P, G, NE])
            top_v = mix("top_v", [P, G, NE])
            top_i = mix("top_i", [P, G, NE], mybir.dt.uint32)
            top_f = mix("top_f", [P, TOP, G])
            onehot = mix("onehot", [P, TOP * G, NE])
            chosen = mix("chosen", [P, G, NE])
            tally_next = mix("tally_next", [P, NE])
            below_top = mix("below_top", [P, G, NE])
            top_e = mix("top_e", [P, G, NE])
            top_sum = mix("top_sum", [P, G])
            top_r = mix("top_r", [P, G])
            place = mix("place", [P, G, NE])
            place_of = mix("place_of", [P, TOP * G, NE])
            slot_f = mix("slot_f", [P, TOP * G])
            slot_i = [mix(f"slot_i{g}", [P, TOP * G], I32) for g in range(2)]

        past = sb("past", [1, NT, NE])
        past_tiles = sb("past_tiles", [1, NT, NE])
        tile_rows = [sb(f"tile_rows{g}", [P, RPT, D]) for g in range(2)]
        slots_moved = sb("slots_moved", [P, NSTEP * TOP * G])
        beyond = sb("beyond", [P, NSTEP * TOP * G, NE - 1])
        w1_now = [sb(f"w1_now{g}", [P, FH + FK]) for g in range(2)]
        w2_now = [sb(f"w2_now{g}", [P, FK + 1, D]) for g in range(2)]
        tile_xT = [sb(f"tile_xT{g}", [P, TR]) for g in range(2)]
        hidden = [sb(f"hidden{g}", [P, FK, TR]) for g in range(2)]
        tile_out = [sb(f"tile_out{g}", [P, RPT, D]) for g in range(2)]
        slot_idx = [sb(f"slot_idx{g}", [P, TOP * G], I32) for g in range(2)]
        expert_rows = [sb(f"expert_rows{g}", [P, TOP * G, D]) for g in range(2)]
        h1_again = [sb(f"h1_again{g}", [P, G, D]) for g in range(2)]
        mixed = sb("mixed", [P, G, D])
        out_rows = [sb(f"out_rows{g}", [P, G, D]) for g in range(2)]

        weights_in = sem("weights_in")
        pe_in = sem("pe_in")
        wup_in = sem("wup_in")
        ids_in = sem("ids_in")
        ident_zero = sem("ident_zero")
        ident_ready = sem("ident_ready")
        zeroed = sem("zeroed")
        moments_done = sem("moments_done")
        spread_done = sem("spread_done")
        rstd_done = sem("rstd_done")
        emb_ready = sem("emb_ready")
        emb_T = sem("emb_T")
        emb_T_kept = sem("emb_T_kept")
        up_done = sem("up_done")
        tx_kept = sem("tx_kept")
        tog_kept = sem("tog_kept")
        tpe_kept = sem("tpe_kept")
        table_out = sem("table_out")
        table_po_out = sem("table_po_out")
        ids_float = sem("ids_float")
        ids_turned = sem("ids_turned")
        ids_ready = sem("ids_ready")

        x_idx_cut = sem("x_idx_cut")
        po_idx_cut = sem("po_idx_cut")
        x_rows_in = sem2("x_rows_in")
        po_rows_in = sem2("po_rows_in")
        xup_T = sem("xup_T")
        xup_kept = sem("xup_kept")
        conv_taps = sem("conv_taps")
        carry_saved = sem("carry_saved")
        xm_ready = sem("xm_ready")
        qk_proj = sem("qk_proj")
        q_kept = sem("q_kept")
        k_kept = sem("k_kept")
        k_T = sem("k_T")
        k_tm_kept = sem("k_tm_kept")
        vg_proj = sem("vg_proj")
        v_kept = sem("v_kept")
        gates_biased = sem("gates_biased")
        gates_exp = sem("gates_exp")
        gates_sig = sem("gates_sig")
        gates_logged = sem("gates_logged")
        gates_T = sem("gates_T")
        row_steps = sem("row_steps")
        m_carried = sem("m_carried")
        row_factors = sem("row_factors")
        stab_out = sem2("stab_out")
        decay_in = sem2("decay_in")
        cols_T = sem("cols_T")
        cols_kept = sem("cols_kept")
        masked = sem("masked")
        v_weighted = sem("v_weighted")
        state_decayed = sem("state_decayed")
        weights_ready = sem("weights_ready")
        scores = sem("scores")
        sd_ready = sem("sd_ready")
        heads_out = sem("heads_out")
        inter_out = sem("inter_out")
        update_out = sem("update_out")
        inter_scaled = sem("inter_scaled")
        out_summed = sem("out_summed")
        state_kept = sem("state_kept")
        den_steps = sem("den_steps")
        h_normed = sem("h_normed")
        h_T = sem("h_T")
        og_T = sem("og_T")
        skip_mixed = sem("skip_mixed")
        y_ready = sem("y_ready")
        down_proj = sem("down_proj")
        h1_summed = sem("h1_summed")
        h1_stored = sem2("h1_stored")

        experts_iota = sem("experts_iota")
        consts_float = sem("consts_float")
        triangle_ready = sem("triangle_ready")
        half_ready = sem("half_ready")
        empty_tiles_out = sem("empty_tiles_out")
        pad_rows_ready = sem("pad_rows_ready")
        pads_out = sem("pads_out")
        totals_out = sem("totals_out")
        sched_steps = sem("sched_steps")
        schedule_ready = sem("schedule_ready")
        ffn_weights_in = sem("ffn_weights_in")
        tile_rows_in = sem2("tile_rows_in")
        tile_T = sem("tile_T")
        tile_T_kept = sem("tile_T_kept")
        w1_picked = sem("w1_picked")
        w2_picked = sem("w2_picked")
        hidden_out = sem("hidden_out")
        gelu_done = sem("gelu_done")
        expert_out = sem("expert_out")
        expert_biased = sem("expert_biased")
        tile_stored = sem2("tile_stored")
        slots_cut = sem("slots_cut")
        h1_back = sem2("h1_back")
        expert_rows_in = sem2("expert_rows_in")
        first_added = sem("first_added")
        combined = sem("combined")
        out_stored = sem2("out_stored")
        ln_steps = sem("ln_steps")
        ln_scaled = sem("ln_scaled")
        xn_ready = sem("xn_ready")
        xn_T = sem("xn_T")
        xn_T_kept = sem("xn_T_kept")
        logits_out = sem("logits_out")
        top_steps = sem("top_steps")
        onehots = sem("onehots")
        onehot_ready = sem("onehot_ready")
        top_exp = sem("top_exp")
        tally_steps = sem("tally_steps")
        tallied = sem("tallied")
        prob_steps = sem("prob_steps")
        ranks_out = sem("ranks_out")
        place_steps = sem("place_steps")
        slots_ready = sem("slots_ready")
        scattered = sem2("scattered")

        block = ctx.enter_context(nc.Block())
        LAST = Step(NC - 1, 1)
        WEIGHTS_IN = 16 * (7 + 2 * KT + 2 * G + 2)

        def steps(slot, engine):
            for peeled in (Step(0, 0), Step(0, 1), Step(1, 0), Step(1, 1), Step(2, 0)):
                slot(peeled)
            with engine.Fori(2, NC - 1) as c:
                slot(Step(c, 1))
                slot(Step(c + 1, 0))
            slot(LAST)

        def own_blocks(v):
            whole = v[:, :, :, :, :, :]
            return bass.AP(whole.tensor, whole.offset, [whole.ap[0], [HPK * HPK * E1, G * KT], [(HPK + 1) * E1, HPK], [1, E1]])

        LAST_TILE = Step(NT // 2 - 1, 1)
        FFN_WEIGHTS_IN = 16 * (3 + FK)

        def is_last_tile(t):
            return t is LAST_TILE

        def tiles(slot, engine):
            for peeled in (Step(0, 0), Step(0, 1)):
                slot(peeled)
            with engine.Fori(1, NT // 2 - 1) as c:
                slot(Step(c, 0))
                slot(Step(c, 1))
            slot(LAST_TILE.prev)
            slot(LAST_TILE)

        def token_steps(slot, engine):
            for peeled in (Step(0, 0), Step(0, 1)):
                slot(peeled)
            with engine.Fori(1, NC - 1) as c:
                slot(Step(c, 0))
                slot(Step(c, 1))
            slot(Step(NC - 1, 0))
            slot(LAST)

        LATER = 6
        AHEAD = 4

        def is_last(st):
            return st is LAST

        @block.sync
        def _(sp):
            sp.dma_start(pe_sb[:, :, :], pe.rearrange("(t p) d -> p t d", p=VR)).then_inc(pe_in, 16)
            sp.dma_start(wup[:, :], w_up).then_inc(wup_in, 16)
            sp.dma_start(ids_i[:, :], x.rearrange("b (c t) -> (b c) t", t=L)).then_inc(ids_in, 16)
            for dst, src in ((wq, w_q), (wk, w_k), (wd, w_down)):
                sp.dma_start(dst[:, :, :], src.rearrange("(k p) n -> p k n", p=P)).then_inc(weights_in, 16)
            for at, n, src in ((0, INNER, w_v), (INNER, NH, w_ig), (INNER + NH, NH, w_fg)):
                sp.dma_start(wvg[:, :, at:at + n], src.rearrange("(k p) n -> p k n", p=P)).then_inc(weights_in, 16)
            sp.dma_start(taps[:, :, :], conv_w.rearrange("(k p) t -> p k t", p=P)).then_inc(weights_in, 16)
            for dst, src in ((convb, conv_b), (skipc, skip)):
                for k in range(KT):
                    sp.dma_start(dst[:, k:k + 1], src[k * P:(k + 1) * P].rearrange("(p o) -> p o", o=1)).then_inc(weights_in, 16)
            for j, src in ((0, b_ig), (1, b_fg)):
                for b in range(G):
                    sp.dma_start(gbias[:, b, j, :], src.partition_broadcast(P)).then_inc(weights_in, 16)
            sp.dma_start(wr[:, :], w_r).then_inc(weights_in, 16)
            sp.dma_start(brb[:, :], b_r.partition_broadcast(P)).then_inc(weights_in, 16)
            sp.wait_ge(tx_kept, VT)
            sp.dma_start(table_x.rearrange("(t p) n -> p t n", p=VR), tx_sb[:, :, :]).then_inc(table_out, 16)
            sp.wait_ge(tog_kept, VT)
            sp.wait_ge(tpe_kept, 1)
            sp.dma_start(table_po.rearrange("(t p) n -> p t n", p=VR), tpo_sb[:, :, :]).then_inc(table_po_out, 16)

            def stabilisers(st):
                wait_apart(sp, (pe_in, 16), (row_factors, 4 * st.n + 4))
                wait_dma(sp, decay_in, st.before)
                sp.dma_start(stab_dram[st.g].rearrange("(r w) -> r w", w=RW), row_stab[:, :]).then_inc(stab_out[st.g], 16)
                wait_dma(sp, stab_out, st)
                wait(sp, heads_out, G, st.before, G)
                sp.dma_start(decay[st.g][:, :, :].rearrange("p r w -> p (r w)"), stab_dram[st.g].partition_broadcast(P)).then_inc(decay_in[st.g], 16)

            def store_h1(st):
                wait(sp, h1_summed, 1, st, 1)
                dst = h1[st.g * G:(st.g + 1) * G, bass.ds(st.c * L, L), :]
                sp.dma_start(dst.rearrange("b t d -> t b d"), h1_sb[st.g][:, :, :]).then_inc(h1_stored[st.g], 16)

            def slot(st):
                if st.prev.exists:
                    store_h1(st.prev)
                if not is_last(st):
                    stabilisers(st.next)

            stabilisers(Step(0, 0))
            sp.dma_start(w1_all[:, :, 0:FH], w1.rearrange("e p n -> p e n")).then_inc(ffn_weights_in, 16)
            sp.dma_start(b1_stage[:, :, :], b1.rearrange("(k p) e -> p k e", p=P)).then_inc(ffn_weights_in, 16)
            for k in range(FK):
                sp.dma_start(w2_all[:, :, k * D:(k + 1) * D], w2[:, k * P:(k + 1) * P, :].rearrange("e p n -> p e n")).then_inc(ffn_weights_in, 16)
            sp.dma_start(w2_all[:, :, FK * D:], b2.partition_broadcast(P)).then_inc(ffn_weights_in, 16)
            sp.wait_ge(zeroed, 1)
            sp.dma_start(slot_in[NE * REGION:SLOT_ROWS, :].rearrange("(r p) d -> p r d", p=P),
                         zero_rows[:, :].unsqueeze(1).broadcast_to([P, (SLOT_ROWS - NE * REGION) // P, D])).then_inc(empty_tiles_out, 16)
            steps(slot, sp)
            store_h1(LAST)
            for g in range(2):
                wait_dma(sp, h1_stored, Step(NC - 1, g))

            sp.wait_ge(pad_rows_ready, 1)
            for e in range(NE):
                row = sp.value_load(pad_row[0:1, e:e + 1], min_val=0, max_val=SLOT_ROWS - TR)
                sp.dma_start(slot_in[bass.ds(row, TR), :].rearrange("(p r) d -> p r d", r=RPT),
                             zero_rows[:, :].unsqueeze(1).broadcast_to([P, RPT, D])).then_inc(pads_out, 16)
            sp.wait_ge(schedule_ready, 1)
            sp.wait_ge(pads_out, 16 * NE)
            sp.wait_ge(empty_tiles_out, 16)
            for g in range(2):
                wait_dma(sp, scattered, Step(NC - 1, g), TOP * G)

            def load_tile(t):
                row = sp.value_load(row_of[0:1, bass.ds(t.n, 1)], min_val=0, max_val=SLOT_ROWS - TR)
                kept = [(tile_T, t.before.n + 1)] if t.before.exists else []
                wait_apart(sp, (schedule_ready, 1), *kept)
                sp.dma_start(tile_rows[t.g][:, :, :], slot_in[bass.ds(row, TR), :].rearrange("(p r) d -> p r d", r=RPT)).then_inc(tile_rows_in[t.g], 16)

            tiles(load_tile, sp)

            def load_h1(st):
                wait(sp, combined, 1, st.before, 1)
                src = h1[st.g * G:(st.g + 1) * G, bass.ds(st.c * L, L), :]
                sp.dma_start(h1_again[st.g][:, :, :], src.rearrange("b t d -> t b d")).then_inc(h1_back[st.g], 16)

            def store_out(st):
                wait(sp, combined, 1, st, 1)
                dst = out[st.g * G:(st.g + 1) * G, bass.ds(st.c * L, L), :]
                sp.dma_start(dst.rearrange("b t d -> t b d"), out_rows[st.g][:, :, :]).then_inc(out_stored[st.g], 16)

            def finish(st):
                load_h1(st)
                if st.prev.exists:
                    store_out(st.prev)

            token_steps(finish, sp)
            store_out(LAST)
            for g in range(2):
                wait_dma(sp, out_stored, Step(NC - 1, g))

        @block.tensor
        def _(pe_):
            T = nc.tensor
            pe_.wait_ge(ident_ready, 1)
            for t in range(VT + 1):
                if t < VT:
                    pe_.wait_ge(emb_ready, t + 1)
                    if t >= 2:
                        pe_.wait_ge(emb_T_kept, t - 1)
                    T.transpose(bank[t % 2][:, 0:VR], emb_n[:, t, :], ident[0:VR, 0:VR]).then_inc(emb_T, 1)
                if t == 0:
                    pe_.wait_ge(wup_in, 16)
                    continue
                pe_.wait_ge(emb_T_kept, t)
                if t >= 3:
                    pe_.wait_ge(tx_kept, t - 2)
                    pe_.wait_ge(tog_kept, t - 2)
                T.matmul(bank[2 + (t - 1) % 2][0:VR, :], emb_nT[:, (t - 1) % 2, :], wup[:, :], start=True, stop=True).then_inc(up_done, 1)
            pe_.wait_ge(ids_float, 1)
            T.transpose(bank[7][:, 0:P], ids_f[:, :], ident[:, :]).then_inc(ids_turned, 1)
            pe_.wait_ge(weights_in, WEIGHTS_IN)

            def turn_x(st):
                wait_dma(pe_, x_rows_in, st, G)
                for k in range(KT):
                    if k == 0:
                        wait(pe_, state_kept, G, st.before, 3)
                    else:
                        wait(pe_, row_steps, 5, st.prev, 1)
                        if st.prev.exists and st.prev.prev.exists and st.prev.prev.prev.exists:
                            wait(pe_, top_steps, 4, st.prev.prev.prev.prev, 1)
                    for b in range(G):
                        last = T.transpose(PJ[k][:, b * L:(b + 1) * L], x_rows[st.g][:, b, k * P:(k + 1) * P], ident[:, :])
                    last.then_inc(xup_T, 1)

            def project_qk(st, w, at):
                for m in range(KT):
                    if (at, m) == (0, 0):
                        wait(pe_, out_summed, G, st.prev, G)
                    elif (at, m) == (0, 1):
                        wait(pe_, inter_scaled, G, st.prev, G)
                    elif m == 0:
                        wait(pe_, state_kept, G, st.prev, G)
                    else:
                        wait(pe_, cols_kept, 1, st, 1)
                        if st.prev.exists and st.prev.prev.exists:
                            wait(pe_, place_steps, 4, st.prev.prev.prev, 1)
                    for k in range(KT):
                        last = T.matmul(SC[at + m][:, :], w[:, k, m * P:(m + 1) * P], xm[st.g][:, k, :], start=k == 0, stop=k == KT - 1)
                    last.then_inc(qk_proj, 1)

            def turn_h(st, tail):
                wait(pe_, h_normed, 1, st, 1)
                for k in range(KT):
                    for b in range(G):
                        last = T.transpose(OX[k][:, b * L:(b + 1) * L], h_tm[:, b, k * P:(k + 1) * P], ident[:, :])
                    last.then_inc(h_T, 1)
                wait_dma(pe_, po_rows_in, st, G)
                for k in range(KT):
                    if not tail:
                        wait(pe_, q_kept, KT, st.next, k + 1)
                    for b in range(G):
                        last = T.transpose(SC[k][:, b * L:(b + 1) * L], po_rows[st.g][:, b, D + k * P:D + (k + 1) * P], ident[:, :])
                    last.then_inc(og_T, 1)

            def turn_k(st):
                wait(pe_, k_kept, KT, st, KT)
                for j in range(2):
                    if not is_last(st):
                        wait(pe_, xup_kept, KT, st.next, j + 1)
                    for b in (2 * j, 2 * j + 1):
                        for k in range(KT):
                            at = (b % 2) * INNER + k * P
                            last = T.transpose(PJ[j][:, at:at + P], kT[:, k, b * L:(b + 1) * L], ident[:, :])
                    last.then_inc(k_T, 1)

            def project_vg(st):
                wait(pe_, xm_ready, KT, st, KT)
                for b in range(G):
                    if b < 2:
                        if st.before.exists:
                            wait(pe_, skip_mixed, KT, st.before, b + 1)
                        else:
                            wait(pe_, v_kept, G, st.prev, G)
                            wait(pe_, gates_biased, G, st.prev, G)
                    else:
                        wait(pe_, gates_biased, G, st, b - 1)
                    for k in range(KT):
                        last = T.matmul(OX[b % 2][:, 0:INNER + 2 * NH], xm[st.g][:, k, b * L:(b + 1) * L], wvg[:, k, :], start=k == 0, stop=k == KT - 1)
                    last.then_inc(vg_proj, 1)

            def project_down(st, tail):
                wait(pe_, y_ready, KT, st, KT)
                if not tail:
                    wait(pe_, k_kept, KT, st.next, 1)
                for b in range(G):
                    for k in range(KT):
                        last = T.matmul(SC[2][:, b * D:(b + 1) * D], y[:, k, b * L:(b + 1) * L], wd[:, k, :], start=k == 0, stop=k == KT - 1)
                last.then_inc(down_proj, 1)

            def score(st, k):
                if k == 0:
                    wait(pe_, q_kept, KT, st, KT)
                    wait(pe_, y_ready, KT, st.prev, KT)
                for pair in ((0, 1), (2, 3)):
                    if k == 0 and pair[0]:
                        wait(pe_, h1_summed, 1, st.prev, 1)
                    if k:
                        wait(pe_, sd_ready, NH, st, pair[1] + 1)
                    for b in range(G):
                        for r in pair:
                            rows = slice(r * DH, (r + 1) * DH)
                            one = T.matmul(SC[r][:, b * L:(b + 1) * L], kT[rows, k, b * L:(b + 1) * L], qT[rows, k, b * L:(b + 1) * L], start=True, stop=True)
                            if b == G - 1:
                                one.then_inc(scores, 1)

            def turn_gates(st):
                wait(pe_, gates_logged, 1, st, 1)
                wait(pe_, k_tm_kept, 2, st.prev, 2)
                for j in range(2):
                    last = T.transpose(PJ[1][0:GH, j * L:(j + 1) * L], gate_log[:, j, :], ident[:, :])
                last.then_inc(gates_T, 1)

            def turn_factors(st):
                wait_apart(pe_, (ident_ready, 1), (row_factors, 4 * st.n + 4))
                if st.prev.exists:
                    wait(pe_, sd_ready, NH, st.prev, NH)
                for j in range(4):
                    last = T.transpose(SC[3][:, j * GH:(j + 1) * GH], row_f[:, j, :], ident[0:GH, 0:GH])
                last.then_inc(cols_T, 1)

            def attend(st, b):
                o, i, u = (OX[0], OX[1], PJ[0]) if b % 2 == 0 else (SC[0], SC[1], SC[2])

                def own(k):
                    for r in range(HPK):
                        last = T.matmul(o[:, k * HPK * E1:(k + 1) * HPK * E1], decay[st.g][:, b * NH + k * HPK + r, 0:L],
                                        v1[st.g][:, b, k, r, :, :].rearrange("p q e -> p (q e)"), start=r == 0, stop=r == HPK - 1)
                    return last

                if b == 0:
                    wait(pe_, sd_ready, NH, st, HPK)
                    if not is_last(st):
                        wait(pe_, v_kept, G, st.next, G)
                        wait(pe_, gates_biased, G, st.next, G)
                if b >= 2:
                    wait(pe_, out_summed, G, st, b - 1)
                own(0)
                wait(pe_, state_kept, G, st.before, b + 1)
                for k in range(KT):
                    last = T.matmul(i[:, k * HPK * E1:(k + 1) * HPK * E1], qT[:, k, b * L:(b + 1) * L],
                                    state[st.g][:, b, k * HPK:(k + 1) * HPK, :].rearrange("p h e -> p (h e)"), start=True, stop=True)
                last.then_inc(inter_out, 1)
                if b == 0:
                    wait(pe_, k_tm_kept, 2, st, 2)
                    wait(pe_, v_weighted, 1, st, 1)
                if b >= 2:
                    wait(pe_, state_kept, G, st, b - 1)
                for k in range(KT):
                    at = b * NH + k * HPK
                    last = T.matmul(u[:, k * HPK * E1:(k + 1) * HPK * E1], k_tm[:, b, k * P:(k + 1) * P],
                                    v_w[:, at:at + HPK, :].rearrange("p h e -> p (h e)"), start=True, stop=True)
                last.then_inc(update_out, 1)
                if b == 0:
                    wait(pe_, sd_ready, NH, st, NH)
                own(1).then_inc(heads_out, 1)

            def turn_xn(st):
                wait(pe_, xn_ready, 1, st, 1)
                if isinstance(st.c, int) and st.n >= 2 * NC - 3:
                    pass
                else:
                    wait(pe_, cols_kept, 1, st.next.next.next, 1)
                for b in range(G):
                    last = T.transpose(SC[3][:, b * L:(b + 1) * L], xn[st.g][:, b, :], ident[:, :])
                last.then_inc(xn_T, 1)

            def route(st):
                wait(pe_, xn_T_kept, 1, st, 1)
                for b in range(G):
                    last = T.matmul(PJ[1][:, b * NE:(b + 1) * NE], xnT[:, b * L:(b + 1) * L], wr[:, :], start=True, stop=True)
                last.then_inc(logits_out, 1)

            def rank(st):
                wait(pe_, onehot_ready, 1, st, 1)
                T.matmul(SC[3][:, 0:G * NE], earlier[:, :], chosen[:, :, :].rearrange("p b e -> p (b e)"), start=True, stop=False)
                T.matmul(SC[3][:, 0:G * NE], ones_pp[:, :], tally[:, 0:G, :].rearrange("p b e -> p (b e)"), start=False, stop=True).then_inc(ranks_out, 1)

            def slot(st):
                nx, pv = st.next, st.prev
                pp = pv.prev if pv.exists else pv
                ppp = pp.prev if pp.exists else pp
                if not is_last(st):
                    turn_x(nx)
                wait(pe_, xm_ready, KT, st, KT)
                project_qk(st, wq, 0)
                if pv.exists:
                    turn_h(pv, False)
                if ppp.exists:
                    rank(ppp)
                project_qk(st, wk, 2)
                if not is_last(st):
                    project_vg(nx)
                if pv.exists:
                    project_down(pv, False)
                turn_k(st)
                score(st, 0)
                if not is_last(st):
                    turn_gates(nx)
                score(st, 1)
                attend(st, 0)
                if not is_last(st):
                    turn_factors(nx)
                attend(st, 1)
                if pp.exists:
                    turn_xn(pp)
                attend(st, 2)
                if pp.exists:
                    route(pp)
                attend(st, 3)

            pe_.wait_ge(zeroed, 2)
            pe_.wait_ge(triangle_ready, 2)
            pe_.wait_ge(consts_float, 1)
            pe_.wait_ge(tx_kept, VT)
            pe_.wait_ge(tog_kept, VT)
            pe_.wait_ge(ids_ready, 1)
            first = Step(0, 0)
            turn_x(first)
            project_vg(first)
            turn_gates(first)
            turn_factors(first)
            steps(slot, pe_)
            turn_h(LAST, True)
            project_down(LAST, True)
            rank(LAST.prev.prev)
            wait(pe_, place_steps, 4, LAST.prev.prev, 1)
            turn_xn(LAST.prev)
            route(LAST.prev)
            rank(LAST.prev)
            wait(pe_, place_steps, 4, LAST.prev, 1)
            turn_xn(LAST)
            wait(pe_, top_steps, 4, LAST.prev, 1)
            route(LAST)
            rank(LAST)
            wait(pe_, place_steps, 4, LAST, 1)
            wait(pe_, tallied, 1, LAST, 1)
            T.matmul(SC[3][:, 0:NE], ones_pp[:, :], tally[:, 0, :], start=True, stop=True).then_inc(totals_out, 1)
            pe_.wait_ge(schedule_ready, 1)
            pe_.wait_ge(ffn_weights_in, FFN_WEIGHTS_IN)

            def turn_tile(t):
                wait_dma(pe_, tile_rows_in, t)
                wait(pe_, tile_T_kept, 1, t.prev, 1)
                for r in range(RPT):
                    last = T.transpose(bank[0][:, r * P:(r + 1) * P], tile_rows[t.g][:, r, :], ident[:, :])
                last.then_inc(tile_T, 1)

            def expand(t):
                wait(pe_, tile_T_kept, 1, t, 1)
                wait(pe_, w1_picked, 1, t, 1)
                for k in range(FK):
                    wait(pe_, gelu_done, FK, t.before, k + 1)
                    T.matmul(bank[2 + 2 * t.g + k][:, :], w1_now[t.g][:, k * P:(k + 1) * P], tile_xT[t.g][:, :], start=True, stop=True).then_inc(hidden_out, 1)

            def contract(t):
                wait(pe_, gelu_done, FK, t, FK)
                wait(pe_, w2_picked, 1, t, 1)
                wait(pe_, expert_biased, 1, t.before, 1)
                for r in range(RPT):
                    for k in range(FK):
                        last = T.matmul(bank[6 + t.g][:, r * P:(r + 1) * P], hidden[t.g][:, k, r * P:(r + 1) * P],
                                        w2_now[t.g][:, k, :], start=k == 0, stop=k == FK - 1)
                last.then_inc(expert_out, 1)

            def mlp(t):
                expand(t)
                if not is_last_tile(t):
                    turn_tile(t.next)
                if t.prev.exists:
                    contract(t.prev)

            turn_tile(Step(0, 0))
            tiles(mlp, pe_)
            contract(LAST_TILE)

        @block.vector
        def _(dve):
            V = nc.vector
            dve.wait_ge(pe_in, 16)
            for t in range(VT):
                last = V.bn_stats(stats[:, t, :], pe_sb[:, t, :])
            last.then_inc(moments_done, 1)
            dve.wait_ge(moments_done, 1)
            for t in range(VT):
                last = V.bn_aggr(moments[:, t, :], stats[:, t, :])
            last.then_inc(moments_done, 1)
            dve.wait_ge(moments_done, 2)
            V.tensor_scalar(spread[:, :], moments[:, :, 1], LN_EPS, None, ALU.add).then_inc(moments_done, 1)
            dve.wait_ge(spread_done, 1)
            V.reciprocal(rstd[:, :], spread[:, :]).then_inc(rstd_done, 1)
            dve.wait_ge(rstd_done, 1)
            for t in range(VT):
                V.tensor_scalar(emb_n[:, t, :], pe_sb[:, t, :], moments[:, t, 0:1], rstd[:, t:t + 1], ALU.subtract, ALU.mult).then_inc(emb_ready, 1)
            for t in range(VT + 1):
                if t < VT:
                    dve.wait_ge(emb_T, t + 1)
                    if t >= 2:
                        dve.wait_ge(up_done, t - 1)
                    V.tensor_copy(emb_nT[:, t % 2, :], bank[t % 2][:, 0:VR]).then_inc(emb_T_kept, 1)
                if t:
                    dve.wait_ge(up_done, t)
                    V.tensor_copy(tx_sb[:, t - 1, :], bank[2 + (t - 1) % 2][0:VR, 0:INNER]).then_inc(tx_kept, 1)
            dve.wait_ge(ids_in, 16)
            V.tensor_copy(ids_f[:, :], ids_i[:, :]).then_inc(ids_float, 1)
            dve.wait_ge(ids_turned, 1)
            V.tensor_copy(ids_T[:, 0:NC, :], bank[7][:, 0:P].rearrange("p (b c) -> p c b", c=NC)).then_inc(ids_ready, 1)
            dve.wait_ge(ids_ready, 1)

            def cut_x_idx(st):
                if st.before.exists:
                    wait_dma(dve, x_rows_in, st.before, G)
                V.tensor_copy(x_idx[st.g][:, :], ids_T[:, bass.ds(st.c, 1), st.g * G:(st.g + 1) * G].rearrange("p c b -> p (c b)")).then_inc(x_idx_cut, 1)

            def cut_po_idx(st):
                if st.before.exists:
                    wait_dma(dve, po_rows_in, st.before, G)
                V.tensor_copy(po_idx[st.g][:, :], ids_T[:, bass.ds(st.c, 1), st.g * G:(st.g + 1) * G].rearrange("p c b -> p (c b)")).then_inc(po_idx_cut, 1)

            def convolve(st):
                done = 0
                for tap in range(TAPS - 2, -1, -1):
                    for k in range(KT):
                        if tap == TAPS - 2:
                            wait(dve, xup_kept, KT, st, k + 1)
                        else:
                            wait(dve, conv_taps, KT * (TAPS - 1), st, done - 1)
                        V.scalar_tensor_tensor(conv[:, k, :, :], xup[st.g][:, k, :, tap:tap + L], taps[:, k, tap:tap + 1],
                                               conv[:, k, :, :], ALU.mult, ALU.add).then_inc(conv_taps, 1)
                        done += 1
                wait(dve, conv_taps, KT * (TAPS - 1), st, KT * (TAPS - 1))
                V.tensor_copy(xup[st.g][:, :, :, 0:TAPS - 1].rearrange("p k b t -> p (k b) t"),
                              xup[st.g][:, :, :, L:L + TAPS - 1].rearrange("p k b t -> p (k b) t")).then_inc(carry_saved, 1)

            def gate_output(st):
                for k in range(KT):
                    wait(dve, h_T, KT, st, k + 1)
                    V.scalar_tensor_tensor(y_s[:, k, :], xm[st.g][:, k, :], skipc[:, k:k + 1], OX[k][:, :], ALU.mult, ALU.add).then_inc(skip_mixed, 1)
                for k in range(KT):
                    wait(dve, og_T, KT, st, k + 1)
                    wait(dve, skip_mixed, KT, st, k + 1)
                    wait(dve, down_proj, 1, st.prev, 1)
                    V.tensor_tensor(y[:, k, :], y_s[:, k, :], SC[k][:, :], ALU.mult).then_inc(y_ready, 1)

            def keep_k_tm(st):
                for j in range(2):
                    wait(dve, k_T, 2, st, j + 1)
                    wait(dve, update_out, G, st.prev, G)
                    V.tensor_copy(k_tm[:, 2 * j:2 * j + 2, :].rearrange("p b n -> p (b n)"), PJ[j][:, :]).then_inc(k_tm_kept, 1)

            def bias_gates(st):
                for b in range(G):
                    wait(dve, v_kept, G, st, b + 1)
                    if b == 0:
                        wait(dve, gates_exp, 1, st.prev, 1)
                    V.tensor_tensor(gates[:, b, :, :], OX[b % 2][:, INNER:INNER + 2 * NH].rearrange("p (j h) -> p j h", j=2), gbias[:, b, :, :], ALU.add).then_inc(gates_biased, 1)

            def add_residual(st):
                wait(dve, down_proj, 1, st, 1)
                wait_dma(dve, h1_stored, st.before)
                V.tensor_tensor(h1_sb[st.g][:, :, :], SC[2][:, :].rearrange("p (b d) -> p b d", b=G), po_rows[st.g][:, :, 0:D], ALU.add).then_inc(h1_summed, 1)

            def sigmoid_gates(st):
                wait(dve, gates_exp, 1, st, 1)
                V.tensor_scalar(gate_d[:, :, :, :], gate_e[:, :, :, :], 1.0, None, ALU.add).then_inc(gates_sig, 1)
                wait(dve, gates_sig, 3, st, 1)
                V.reciprocal(gate_r[:, :, :, :], gate_d[:, :, :, :]).then_inc(gates_sig, 1)
                wait(dve, gates_sig, 3, st, 2)
                wait(dve, gates_logged, 1, st.prev, 1)
                V.tensor_scalar(gate_s[:, :, :, :], gate_r[:, :, :, :], GATE_EPS, None, ALU.add).then_inc(gates_sig, 1)

            def weigh_scores(st, heads):
                for h in heads:
                    k, r = divmod(h, HPK)
                    wait(dve, weights_ready, NH, st, h + 1)
                    wait(dve, scores, NH, st, h + 1)
                    e = decay[st.g][:, :, 0:L].rearrange("p (b h) t -> p h b t", h=NH)[:, h]
                    V.tensor_tensor(e, SC[r][:, :].rearrange("p (b t) -> p b t", b=G), e, ALU.mult).then_inc(sd_ready, 1)

            def gate_rows(st):
                wait(dve, gates_T, 1, st, 1)
                V.tensor_copy(rows_if[:, :, :], PJ[1][0:GH, 0:2 * L].rearrange("p (j t) -> p j t", j=2)).then_inc(row_steps, 1)
                wait(dve, row_steps, 5, st, 1)
                V.tensor_tensor_scan(row_b[:, :], ones_row[:, :], rows_if[:, 1, :], 0.0, ALU.mult, ALU.add).then_inc(row_steps, 1)
                wait(dve, m_carried, 1, st.before, 1)
                wait(dve, row_factors, 4, st.prev, 4)
                V.tensor_tensor_scan(row_m[:, :], rows_if[:, 1, :], rows_if[:, 0, :], m_carry[st.g][:, 0:1], ALU.add, ALU.max).then_inc(row_steps, 1)
                wait(dve, row_steps, 5, st, 2)
                wait(dve, cols_T, 1, st.prev, 1)
                V.tensor_tensor(row_f[:, 0, :], rows_if[:, 0, :], row_b[:, :], ALU.subtract).then_inc(row_steps, 1)
                wait(dve, row_steps, 5, st, 3)
                wait_dma(dve, stab_out, st.prev)
                V.tensor_tensor(row_stab[:, 0:L], row_b[:, :], row_m[:, :], ALU.subtract).then_inc(row_steps, 1)

            def keep_factors(st):
                wait(dve, row_factors, 4, st, 4)
                V.tensor_copy(m_carry[st.g][:, :], row_m[:, L - 1:L]).then_inc(m_carried, 1)
                wait(dve, cols_T, 1, st, 1)
                wait(dve, v_weighted, 1, st.before, 1)
                V.tensor_copy(cols[st.g][:, :, :], SC[3][:, 0:4 * GH].rearrange("p (j r) -> p j r", j=4)).then_inc(cols_kept, 1)

            def sum_heads(st, b):
                o, i, u = (OX[0], OX[1], PJ[0]) if b % 2 == 0 else (SC[0], SC[1], SC[2])
                hs = slice(b * NH, (b + 1) * NH)
                wait(dve, inter_out, G, st, b + 1)
                if b:
                    wait(dve, out_summed, G, st, b)
                else:
                    wait(dve, h_normed, 1, st.prev, 1)
                V.tensor_tensor(inter[:, :, :], i[:, 0:NH * E1].rearrange("p (h e) -> p h e", h=NH),
                                cols[st.g][:, 1, hs].unsqueeze(2).broadcast_to([P, NH, E1]), ALU.mult).then_inc(inter_scaled, 1)
                wait(dve, inter_scaled, G, st, b + 1)
                wait(dve, heads_out, G, st, b + 1)
                V.tensor_tensor(osum[:, b, :, :], o[:, 0:NH * E1].rearrange("p (h e) -> p h e", h=NH), inter[:, :, :], ALU.add).then_inc(out_summed, 1)
                wait(dve, update_out, G, st, b + 1)
                wait(dve, state_decayed, 1, st, 1)
                uv = u[:, 0:NH * E1].rearrange("p (k r e) -> p r k e", k=KT, r=HPK)
                sv = state[st.g][:, b, :, :].rearrange("p (k r) e -> p r k e", k=KT)
                dv = state_d[:, b, :, :].rearrange("p (k r) e -> p r k e", k=KT)
                for r in range(HPK):
                    rows = slice(r * DH, (r + 1) * DH)
                    last = V.tensor_tensor(sv[rows, r], uv[rows, r], dv[rows, r], ALU.add)
                last.then_inc(state_kept, 1)

            def normalise(st):
                wait(dve, out_summed, G, st, G)
                dot = osum[:, :, :, DH].rearrange("p b h -> p (b h)")
                V.scalar_tensor_tensor(den[:, 0, :], dot, -1.0, dot, ALU.mult, ALU.max).then_inc(den_steps, 1)
                wait(dve, den_steps, 4, st, 1)
                V.tensor_tensor(den[:, 1, :], den[:, 0, :], cols[st.g][:, 2, :], ALU.max).then_inc(den_steps, 1)
                wait(dve, den_steps, 4, st, 2)
                V.tensor_scalar(den[:, 2, :], den[:, 1, :], GATE_EPS, None, ALU.add).then_inc(den_steps, 1)
                wait(dve, den_steps, 4, st, 3)
                V.reciprocal(den[:, 3, :], den[:, 2, :]).then_inc(den_steps, 1)
                wait(dve, den_steps, 4, st, 4)
                wait(dve, h_T, KT, st.prev, KT)
                V.tensor_tensor(h_tm[:, :, :].rearrange("p b (h e) -> p (b h) e", h=NH), osum[:, :, :, 0:DH].rearrange("p b h e -> p (b h) e"),
                                den[:, 3, :].unsqueeze(2).broadcast_to([P, GH, DH]), ALU.mult).then_inc(h_normed, 1)

            def row_moments(st):
                wait(dve, h1_summed, 1, st, 1)
                for b in range(G):
                    last = V.bn_stats(ln_stats[:, b, :], h1_sb[st.g][:, b, :])
                last.then_inc(ln_steps, 1)
                wait_apart(dve, (zeroed, 2), (ln_steps, 3 * st.n + 1))
                for b in range(G):
                    last = V.bn_aggr(ln_mv[:, b, :], ln_stats[:, b, :])
                last.then_inc(ln_steps, 1)
                wait(dve, ln_steps, 3, st, 2)
                V.tensor_scalar(ln_var[:, :], ln_mv[:, :, 1], LN_EPS, None, ALU.add).then_inc(ln_steps, 1)

            def normalise_rows(st):
                wait(dve, ln_scaled, 1, st, 1)
                wait_dma(dve, scattered, st.before, TOP * G)
                for b in range(G):
                    last = V.tensor_scalar(xn[st.g][:, b, :], h1_sb[st.g][:, b, :], ln_mv[:, b, 0:1], ln_rstd[:, b:b + 1], ALU.subtract, ALU.mult)
                last.then_inc(xn_ready, 1)

            def keep_logits(st):
                wait(dve, logits_out, 1, st, 1)
                V.tensor_tensor(logits[:, :, :], PJ[1][:, 0:G * NE].rearrange("p (b e) -> p b e", b=G), brb[:, :].unsqueeze(1).broadcast_to([P, G, NE]), ALU.add).then_inc(top_steps, 1)

            def choose(st):
                kept = [(prob_steps, 3 * st.prev.n + 3)] if st.prev.exists else []
                wait_apart(dve, (zeroed, 2), (top_steps, 4 * st.n + 1), *kept)
                for b in range(G):
                    last = V.max(top_v[:, b, :], logits[:, b, :])
                last.then_inc(top_steps, 1)
                wait_apart(dve, (zeroed, 2), (top_steps, 4 * st.n + 2))
                for b in range(G):
                    last = V.max_index(top_i[:, b, :], top_v[:, b, :], logits[:, b, :])
                last.then_inc(top_steps, 1)
                V.tensor_tensor(below_top[:, :, :], top_v[:, :, :], top_v[:, :, 0:1].broadcast_to([P, G, NE]), ALU.subtract).then_inc(top_steps, 1)
                wait(dve, top_steps, 4, st, 3)
                V.tensor_copy(top_f[:, :, :], top_i[:, :, 0:TOP].rearrange("p b k -> p k b")).then_inc(onehots, 1)
                wait(dve, onehots, 3, st, 1)
                V.tensor_tensor(onehot[:, :, :], expert_f[:, :].unsqueeze(1).broadcast_to([P, TOP * G, NE]),
                                top_f[:, :, :].rearrange("p k b -> p (k b)").unsqueeze(2).broadcast_to([P, TOP * G, NE]), ALU.is_equal).then_inc(onehots, 1)
                wait(dve, onehots, 3, st, 2)
                V.tensor_tensor(chosen[:, :, :], onehot[:, 0:G, :], onehot[:, G:2 * G, :], ALU.add).then_inc(onehots, 1)
                wait(dve, onehots, 3, st, 3)
                for b in range(1, G):
                    one = V.tensor_tensor(tally[:, b, :], tally[:, b - 1, :], chosen[:, b - 1, :], ALU.add).then_inc(tally_steps, 1)
                    if b < G - 1:
                        wait(dve, tally_steps, G - 1, st, b)
                wait(dve, tally_steps, G - 1, st, G - 1)
                V.tensor_tensor(tally_next[:, :], tally[:, G - 1, :], chosen[:, G - 1, :], ALU.add).then_inc(onehot_ready, 1)

            def probabilities(st):
                wait(dve, top_exp, 1, st, 1)
                V.reduce_sum(top_sum[:, :], top_e[:, :, :], mybir.AxisListType.X).then_inc(prob_steps, 1)
                wait(dve, prob_steps, 3, st, 1)
                V.reciprocal(top_r[:, :], top_sum[:, :]).then_inc(prob_steps, 1)
                wait(dve, prob_steps, 3, st, 2)
                V.tensor_tensor(probs_all[:, bass.ds(st.n, 1), :].rearrange("p o (k b) -> p (o k) b", k=TOP), top_e[:, :, 0:TOP].rearrange("p b k -> p k b"),
                                top_r[:, :].unsqueeze(1).broadcast_to([P, TOP, G]), ALU.mult).then_inc(prob_steps, 1)

            def place_rows(st):
                wait(dve, ranks_out, 1, st, 1)
                V.tensor_tensor(place[:, :, :], SC[3][:, 0:G * NE].rearrange("p (b e) -> p b e", b=G), region_f[:, :].unsqueeze(1).broadcast_to([P, G, NE]), ALU.add).then_inc(place_steps, 1)
                V.tensor_copy(tally[:, 0, :], tally_next[:, :]).then_inc(tallied, 1)

            def place_tokens(st):
                wait(dve, place_steps, 4, st, 1)
                V.tensor_tensor(place_of[:, :, :].rearrange("p (k b) e -> p k (b e)", k=TOP), onehot[:, :, :].rearrange("p (k b) e -> p k (b e)", k=TOP),
                                place[:, :, :].rearrange("p b e -> p (b e)").unsqueeze(1).broadcast_to([P, TOP, G * NE]), ALU.mult).then_inc(place_steps, 1)
                wait(dve, place_steps, 4, st, 2)
                V.reduce_sum(slot_f[:, :], place_of[:, :, :], mybir.AxisListType.X).then_inc(place_steps, 1)
                wait(dve, place_steps, 4, st, 3)
                V.tensor_copy(slot_i[st.g][:, :], slot_f[:, :]).then_inc(slots_ready, 1)
                V.tensor_copy(slots_all[:, bass.ds(st.n, 1), :].rearrange("p o k -> p (o k)"), slot_f[:, :]).then_inc(place_steps, 1)

            def slot(st):
                nx, pv = st.next, st.prev
                pp = pv.prev if pv.exists else pv
                ppp = pp.prev if pp.exists else pp
                cut_po_idx(st)
                if not is_last(st):
                    cut_x_idx(st.after)
                if ppp.exists:
                    choose(ppp)
                if not is_last(st):
                    convolve(nx)
                if ppp.exists:
                    place_rows(ppp)
                if pv.exists:
                    gate_output(pv)
                if pp.exists:
                    row_moments(pp)
                if ppp.exists:
                    place_tokens(ppp)
                    probabilities(ppp)
                if not is_last(st):
                    bias_gates(nx)
                if pv.exists:
                    add_residual(pv)
                keep_k_tm(st)
                if not is_last(st):
                    sigmoid_gates(nx)
                weigh_scores(st, range(0, 4))
                if not is_last(st):
                    gate_rows(nx)
                weigh_scores(st, range(4, 8))
                if pp.exists:
                    normalise_rows(pp)
                sum_heads(st, 0)
                if not is_last(st):
                    keep_factors(nx)
                sum_heads(st, 1)
                sum_heads(st, 2)
                if pp.exists:
                    keep_logits(pp)
                sum_heads(st, 3)
                normalise(st)

            first = Step(0, 0)
            cut_x_idx(first)
            cut_x_idx(first.next)
            V.memset(ones_row[:, :], 1.0)
            V.memset(ones_pp[:, :], 1.0)
            V.memset(zero_rows[:, :], 0.0)
            V.memset(ones_e[:, :], 1.0)
            V.memset(tally[:, :, :], 0.0)
            V.memset(minus_half[:, :], -0.5)
            V.memset(ids_T[:, NC, :], 0)
            for g in range(2):
                V.memset(xup[g][:, :, :, 0:TAPS - 1], 0.0)
                V.memset(v1[g][:, :, :, :, :, :].rearrange("p b k r q e -> p (b k r q e)"), 0.0)
                V.memset(m_carry[g][:, :], 0.0)
                last = V.memset(state[g][:, :, :, :], 0.0)
            last.then_inc(zeroed, 1)
            dve.wait_ge(zeroed, 1)
            for g in range(2):
                last = V.memset(own_blocks(v1[g])[:, :, :, DH:E1], 1.0)
            last.then_inc(zeroed, 1)
            dve.wait_ge(zeroed, 2)
            dve.wait_ge(weights_in, WEIGHTS_IN)
            dve.wait_ge(experts_iota, 3)
            V.tensor_copy(expert_f[:, :], expert_i[:, :])
            V.tensor_copy(region_f[:, :], region_i[:, :])
            V.tensor_copy(tile_f[:, :], tile_i[:, :]).then_inc(consts_float, 1)
            dve.wait_ge(consts_float, 1)
            convolve(first)
            bias_gates(first)
            sigmoid_gates(first)
            gate_rows(first)
            keep_factors(first)
            steps(slot, dve)
            gate_output(LAST)
            add_residual(LAST)
            row_moments(LAST.prev)
            choose(LAST.prev.prev)
            place_rows(LAST.prev.prev)
            place_tokens(LAST.prev.prev)
            probabilities(LAST.prev.prev)
            normalise_rows(LAST.prev)
            row_moments(LAST)
            for st in (LAST.prev, LAST):
                keep_logits(st)
                choose(st)
                place_rows(st)
                place_tokens(st)
                probabilities(st)
                if st is not LAST:
                    normalise_rows(LAST)
            dve.wait_ge(totals_out, 1)
            V.tensor_copy(total[:, :], SC[3][:, 0:NE]).then_inc(sched_steps, 1)
            dve.wait_ge(sched_steps, 1)
            V.tensor_tensor(pad_row[:, :], total[0:1, :], region_f[0:1, :], ALU.add).then_inc(pad_rows_ready, 1)
            V.tensor_scalar(total_up[:, :], total[:, :], float(TR - 1), None, ALU.add).then_inc(sched_steps, 1)
            dve.wait_ge(sched_steps, 2)
            V.tensor_scalar(tiles_i[:, :], total_up[:, :], TILE_SHIFT, None, ALU.logical_shift_right).then_inc(sched_steps, 1)
            dve.wait_ge(sched_steps, 3)
            V.tensor_copy(tiles_f[:, :], tiles_i[:, :]).then_inc(sched_steps, 1)
            dve.wait_ge(sched_steps, 4)
            V.tensor_tensor_scan(tiles_end[:, :], ones_e[:, :], tiles_f[0:1, :], 0.0, ALU.mult, ALU.add).then_inc(sched_steps, 1)
            dve.wait_ge(sched_steps, 5)
            V.tensor_tensor(past[:, :, :], tile_f[:, :].unsqueeze(2).broadcast_to([1, NT, NE]), tiles_end[:, :].unsqueeze(1).broadcast_to([1, NT, NE]), ALU.is_ge).then_inc(sched_steps, 1)
            dve.wait_ge(sched_steps, 6)
            V.tensor_tensor(past_tiles[:, :, :], past[:, :, :], tiles_f[0:1, :].unsqueeze(1).broadcast_to([1, NT, NE]), ALU.mult)
            V.reduce_sum(tile_expert[:, :], past[:, :, :], mybir.AxisListType.X).then_inc(sched_steps, 1)
            dve.wait_ge(sched_steps, 7)
            V.reduce_sum(tile_start[:, :], past_tiles[:, :, :], mybir.AxisListType.X).then_inc(sched_steps, 1)
            V.tensor_scalar(expert_of[:, :], tile_expert[:, :], float(NE - 1), None, ALU.min)
            V.tensor_scalar(tile_base[:, :], tile_expert[:, :], float(REGION), None, ALU.mult)
            dve.wait_ge(sched_steps, 8)
            V.tensor_tensor(tile_in[:, :], tile_f[:, :], tile_start[:, :], ALU.subtract).then_inc(sched_steps, 1)
            dve.wait_ge(sched_steps, 9)
            V.scalar_tensor_tensor(row_of[:, :], tile_in[:, :], float(TR), tile_base[:, :], ALU.mult, ALU.add).then_inc(schedule_ready, 1)
            dve.wait_ge(ffn_weights_in, FFN_WEIGHTS_IN)

            def keep_tile(t):
                wait(dve, tile_T, 1, t, 1)
                wait(dve, hidden_out, FK, t.before, FK)
                V.tensor_copy(tile_xT[t.g][:, :], bank[0][:, :]).then_inc(tile_T_kept, 1)

            def bias_expert(t):
                wait(dve, expert_out, 1, t, 1)
                wait_dma(dve, tile_stored, t.before)
                V.tensor_tensor(tile_out[t.g][:, :, :], bank[6 + t.g][:, :].rearrange("p (r d) -> p r d", r=RPT),
                                w2_now[t.g][:, FK:FK + 1, :].broadcast_to([P, RPT, D]), ALU.add).then_inc(expert_biased, 1)

            def expert_number(t):
                return dve.value_load(expert_of[0:1, bass.ds(t.n, 1)], min_val=0, max_val=NE - 1)

            def pick_w1(t, e):
                wait(dve, gelu_done, FK, t.before, FK)
                V.tensor_copy(w1_now[t.g][:, :], w1_all[:, bass.ds(e, 1), :].rearrange("p o n -> p (o n)")).then_inc(w1_picked, 1)

            def pick_w2(t, e):
                wait(dve, expert_biased, 1, t.before, 1)
                V.tensor_copy(w2_now[t.g][:, :, :].rearrange("p k n -> p (k n)"), w2_all[:, bass.ds(e, 1), :].rearrange("p o n -> p (o n)")).then_inc(w2_picked, 1)

            def mlp(t):
                if not is_last_tile(t):
                    e = expert_number(t.next)
                    pick_w1(t.next, e)
                    keep_tile(t.next)
                if t.prev.exists:
                    bias_expert(t.prev)
                if not is_last_tile(t):
                    pick_w2(t.next, e)

            for k in range(FK):
                last = V.tensor_copy(w1_all[:, :, FH + k], b1_stage[:, k, :])
            last.then_inc(sched_steps, 1)
            dve.wait_ge(sched_steps, 10)
            slots = slots_all[:, :, :].rearrange("p s k -> p (s k)")
            wide = [P, NSTEP * TOP * G, NE - 1]
            V.tensor_scalar(shift[:, :], tiles_f[:, :], float(TR), float(-REGION), ALU.mult, ALU.add)
            V.tensor_tensor(beyond[:, :, :], slots.unsqueeze(2).broadcast_to(wide), region_f[:, 1:NE].unsqueeze(1).broadcast_to(wide), ALU.is_ge).then_inc(sched_steps, 1)
            dve.wait_ge(sched_steps, 11)
            V.tensor_tensor(beyond[:, :, :], beyond[:, :, :], shift[:, 0:NE - 1].unsqueeze(1).broadcast_to(wide), ALU.mult).then_inc(sched_steps, 1)
            dve.wait_ge(sched_steps, 12)
            V.reduce_sum(slots_moved[:, :], beyond[:, :, :], mybir.AxisListType.X).then_inc(sched_steps, 1)
            dve.wait_ge(sched_steps, 13)
            V.tensor_tensor(out_slots[:, :, :].rearrange("p s k -> p (s k)"), slots_moved[:, :], slots, ALU.add).then_inc(sched_steps, 1)
            dve.wait_ge(sched_steps, 14)
            e = expert_number(Step(0, 0))
            pick_w1(Step(0, 0), e)
            keep_tile(Step(0, 0))
            pick_w2(Step(0, 0), e)
            tiles(mlp, dve)
            bias_expert(LAST_TILE)

            def cut_slots(st):
                if st.before.exists:
                    wait_dma(dve, expert_rows_in, st.before, TOP * G)
                V.tensor_copy(slot_idx[st.g][:, :], out_slots[:, bass.ds(st.n, 1), :].rearrange("p o k -> p (o k)")).then_inc(slots_cut, 1)

            def combine(st):
                wait_dma(dve, expert_rows_in, st, TOP * G)
                wait_dma(dve, h1_back, st)
                wait_dma(dve, out_stored, st.before)
                wait(dve, combined, 1, st.prev, 1)
                for b in range(G):
                    last = V.scalar_tensor_tensor(mixed[:, b, :], expert_rows[st.g][:, b, :], probs_all[:, bass.ds(st.n, 1), b], h1_again[st.g][:, b, :], ALU.mult, ALU.add)
                last.then_inc(first_added, 1)
                wait(dve, first_added, 1, st, 1)
                for b in range(G):
                    last = V.scalar_tensor_tensor(out_rows[st.g][:, b, :], expert_rows[st.g][:, G + b, :], probs_all[:, bass.ds(st.n, 1), G + b], mixed[:, b, :], ALU.mult, ALU.add)
                last.then_inc(combined, 1)

            def finish(st):
                cut_slots(st)
                if st.prev.exists:
                    combine(st.prev)

            token_steps(finish, dve)
            combine(LAST)

        @block.scalar
        def _(act):
            A = nc.scalar
            act.wait_ge(moments_done, 3)
            A.activation(spread[:, :], spread[:, :], ACT.Sqrt).then_inc(spread_done, 1)
            for t in range(VT):
                act.wait_ge(tx_kept, t + 1)
                A.activation(tpo_sb[:, t, D:PO], bank[2 + t % 2][0:VR, INNER:2 * INNER], ACT.Silu).then_inc(tog_kept, 1)
            act.wait_ge(weights_in, WEIGHTS_IN)
            act.wait_ge(zeroed, 2)

            def keep_x(st):
                for k in range(KT):
                    src = PJ[k][:, :].rearrange("p (b t) -> p b t", b=G)
                    wait(act, xup_T, KT, st, k + 1)
                    wait(act, carry_saved, 1, st.before, 1)
                    A.activation(xup[st.g][:, k, :, TAPS - 1:], src, ACT.Copy)
                    wait(act, xm_ready, KT, st.prev, k + 1)
                    A.activation(conv[:, k, :, :], src, ACT.Identity, bias=convb[:, k:k + 1], scale=taps[:, k, TAPS - 1:TAPS]).then_inc(xup_kept, 1)

            def keep_q(st):
                for m in range(KT):
                    wait(act, qk_proj, 2 * KT, st, m + 1)
                    wait(act, inter_out, G, st.prev, G)
                    A.activation(qT[:, m, :], SC[m][:, :], ACT.Copy, scale=float(DH) ** -0.5).then_inc(q_kept, 1)

            def keep_k(st):
                for m in range(KT):
                    wait(act, qk_proj, 2 * KT, st, KT + m + 1)
                    A.activation(kT[:, m, :], SC[2 + m][:, :], ACT.Copy).then_inc(k_kept, 1)

            def silu_x(st):
                for k in range(KT):
                    wait(act, conv_taps, KT * (TAPS - 1), st, KT * (TAPS - 2) + k + 1)
                    wait(act, skip_mixed, KT, st.before, k + 1)
                    A.activation(xm[st.g][:, k, :], conv[:, k, :, :].rearrange("p b t -> p (b t)"), ACT.Silu).then_inc(xm_ready, 1)

            def keep_v(st):
                for b in range(G):
                    wait(act, vg_proj, G, st, b + 1)
                    if b == 0:
                        wait(act, heads_out, G, st.before, G)
                        wait(act, v_weighted, 1, st.before, 1)
                    A.activation(own_blocks(v1[st.g])[:, KT * b:KT * (b + 1), :, 0:DH], OX[b % 2][:, 0:INNER].rearrange("p (k r e) -> p k r e", k=KT, r=HPK), ACT.Copy).then_inc(v_kept, 1)

            def exp_gates(st):
                wait(act, gates_biased, G, st, G)
                A.activation(gate_e[:, :, :, :].rearrange("p b j h -> p (b j h)"), gates[:, :, :, :].rearrange("p b j h -> p (b j h)"), ACT.Exp, scale=-1.0).then_inc(gates_exp, 1)

            def log_gates(st):
                wait(act, gates_sig, 3, st, 3)
                wait(act, gates_T, 1, st.prev, 1)
                A.activation(gate_log[:, :, :].rearrange("p j (b h) -> p j b h", b=G), gate_s[:, :, :, :].rearrange("p b j h -> p j b h"), ACT.Ln).then_inc(gates_logged, 1)

            def exp_weights(st, heads):
                for h in heads:
                    if h == 0:
                        wait(act, cols_kept, 1, st, 1)
                        wait(act, masked, 2, st, 2)
                    for b in range(G):
                        e = decay[st.g][:, b * NH + h, 0:L]
                        last = A.activation(e, e, ACT.Exp, bias=cols[st.g][:, 0, b * NH + h:b * NH + h + 1])
                    last.then_inc(weights_ready, 1)

            def exp_rows(st):
                wait(act, row_steps, 5, st, 5)
                wait(act, cols_T, 1, st.prev, 1)
                A.activation(row_f[:, 1, :], row_stab[:, 0:L], ACT.Exp, bias=m_carry[st.g][:, 0:1]).then_inc(row_factors, 1)
                A.activation(row_stab[:, L:RW], row_stab[:, L - 1:L], ACT.Exp, bias=m_carry[st.g][:, 0:1]).then_inc(row_factors, 1)
                A.activation(row_f[:, 2, :], row_m[:, :], ACT.Exp, scale=-1.0).then_inc(row_factors, 1)
                A.activation(row_f[:, 3, :], row_f[:, 0, :], ACT.Exp, bias=row_stab[:, L - 1:L]).then_inc(row_factors, 1)

            def keep_xn(st):
                wait(act, xn_T, 1, st, 1)
                wait(act, logits_out, 1, st.prev, 1)
                A.activation(xnT[:, :], SC[3][:, :], ACT.Copy).then_inc(xn_T_kept, 1)

            def exp_top(st):
                wait(act, top_steps, 4, st, 4)
                wait(act, prob_steps, 3, st.prev, 3)
                A.activation(top_e[:, :, :].rearrange("p b e -> p (b e)"), below_top[:, :, :].rearrange("p b e -> p (b e)"), ACT.Exp).then_inc(top_exp, 1)

            def slot(st):
                nx, pv = st.next, st.prev
                pp = pv.prev if pv.exists else pv
                ppp = pp.prev if pp.exists else pp
                if not is_last(st):
                    keep_x(nx)
                started = st.n if isinstance(st.n, int) else 1
                if started:
                    exp_weights(st, range(AHEAD, LATER))
                keep_q(st)
                if ppp.exists:
                    exp_top(ppp)
                if not is_last(st):
                    silu_x(nx)
                keep_k(st)
                if not is_last(st):
                    keep_v(nx)
                    exp_gates(nx)
                exp_weights(st, range(LATER if started else 0, NH))
                if not is_last(st):
                    log_gates(nx)
                    exp_rows(nx)
                if pp.exists:
                    keep_xn(pp)
                if not is_last(st):
                    exp_weights(nx, range(0, AHEAD))

            first = Step(0, 0)
            keep_x(first)
            silu_x(first)
            keep_v(first)
            exp_gates(first)
            log_gates(first)
            exp_rows(first)
            steps(slot, act)
            exp_top(LAST.prev.prev)
            for st in (LAST.prev, LAST):
                keep_xn(st)
                exp_top(st)
            act.wait_ge(schedule_ready, 1)
            act.wait_ge(ffn_weights_in, FFN_WEIGHTS_IN)

            def bend(t):
                for k in range(FK):
                    wait(act, hidden_out, FK, t, k + 1)
                    if k == 0:
                        wait(act, expert_out, 1, t.before, 1)
                    A.activation(hidden[t.g][:, k, :], bank[2 + 2 * t.g + k][:, :], ACT.Gelu,
                                 bias=w1_now[t.g][:, FH + k:FH + k + 1]).then_inc(gelu_done, 1)

            tiles(bend, act)

        @block.gpsimd
        def _(pool):
            Q = nc.gpsimd
            Q.memset(ident[:, :], 0.0).then_inc(ident_zero, 1)
            pool.wait_ge(ident_zero, 1)
            Q.affine_select(out=ident[:, :], in_=ident[:, :], compare_op=ALU.not_equal, fill=1.0, base=0,
                            pattern=[[-1, P]], channel_multiplier=1).then_inc(ident_ready, 1)
            Q.iota(expert_i[:, :], pattern=[[1, NE]], base=0, channel_multiplier=0).then_inc(experts_iota, 1)
            Q.iota(region_i[:, :], pattern=[[REGION, NE]], base=0, channel_multiplier=0).then_inc(experts_iota, 1)
            Q.iota(tile_i[:, :], pattern=[[1, NT]], base=0, channel_multiplier=0).then_inc(experts_iota, 1)
            Q.memset(earlier[:, :], 1.0).then_inc(triangle_ready, 1)
            pool.wait_ge(triangle_ready, 1)
            Q.affine_select(out=earlier[:, :], in_=earlier[:, :], compare_op=ALU.is_gt, fill=0.0, base=0,
                            pattern=[[1, P]], channel_multiplier=-1).then_inc(triangle_ready, 1)
            pool.wait_ge(pe_in, 16)
            Q.tensor_copy(tpo_sb[:, :, 0:D], pe_sb[:, :, :]).then_inc(tpe_kept, 1)
            pool.wait_ge(table_out, 16)

            def gather(rows, table, idx, sems, st):
                for b in range(G):
                    Q.indirect_dma_start(out=rows[st.g][:, b, :], out_offset=None, in_=table[:, :],
                                         in_offset=bass.IndirectOffsetOnAxis(ap=idx[st.g][:, b:b + 1], axis=0)).then_inc(sems[st.g], 16)

            def gather_x(st):
                kept = [(xup_T, KT * st.before.n + KT)] if st.before.exists else []
                wait_apart(pool, (table_out, 16), (x_idx_cut, st.n + 1), *kept)
                gather(x_rows, table_x, x_idx, x_rows_in, st)

            def gather_po(st):
                kept = [(h1_summed, st.before.n + 1)] if st.before.exists else []
                wait_apart(pool, (table_po_out, 16), (po_idx_cut, st.n + 1), *kept)
                gather(po_rows, table_po, po_idx, po_rows_in, st)

            def mask(st):
                wait_apart(pool, (ident_ready, 1), (decay_in[st.g], 16 * (st.c + 1)))
                for j in range(2):
                    m = decay[st.g][:, j * GH // 2:(j + 1) * GH // 2, 0:L]
                    Q.affine_select(out=m, in_=m, compare_op=ALU.is_ge, fill=MASKED, base=0,
                                    pattern=[[0, GH // 2], [1, L]], channel_multiplier=-1).then_inc(masked, 1)

            def scale_rows(st):
                wait(pool, ln_steps, 3, st, 3)
                wait(pool, xn_ready, 1, st.prev, 1)
                Q.tensor_tensor(ln_rstd[:, :], ln_var[:, :], minus_half[:, :], ALU.pow).then_inc(ln_scaled, 1)

            def scatter_rows(st):
                wait_apart(pool, (triangle_ready, 2), (slots_ready, st.n + 1))
                for j in range(TOP * G):
                    Q.indirect_dma_start(out=slot_in[:, :], out_offset=bass.IndirectOffsetOnAxis(ap=slot_i[st.g][:, j:j + 1], axis=0),
                                         in_=xn[st.g][:, j % G, :], in_offset=None).then_inc(scattered[st.g], 16)

            def slot(st):
                pp = st.prev.prev if st.prev.exists else st.prev
                ppp = pp.prev if pp.exists else pp
                wait(pool, cols_kept, 1, st, 1)
                wait(pool, v_kept, G, st, G)
                wait(pool, update_out, G, st.prev, G)
                Q.tensor_tensor(v_w[:, :, :].rearrange("p (m r) e -> p m r e", r=HPK), own_blocks(v1[st.g]),
                                cols[st.g][:, 3, :].rearrange("p (m r) -> p m r", r=HPK).unsqueeze(3).broadcast_to([P, G * KT, HPK, E1]), ALU.mult).then_inc(v_weighted, 1)
                wait(pool, state_kept, G, st.prev, G)
                Q.tensor_tensor(state_d[:, :, :, :].rearrange("p b h e -> p (b h) e"), state[st.g][:, :, :, :].rearrange("p b h e -> p (b h) e"),
                                decay[st.g][:, :, L:RW].broadcast_to([P, GH, E1]), ALU.mult).then_inc(state_decayed, 1)
                gather_po(st)
                if pp.exists:
                    scale_rows(pp)
                if not is_last(st):
                    gather_x(st.after)
                if ppp.exists:
                    scatter_rows(ppp)
                if not is_last(st):
                    mask(st.next)

            first = Step(0, 0)
            gather_x(first)
            gather_x(first.next)
            mask(first)
            steps(slot, pool)
            scale_rows(LAST.prev)
            scatter_rows(LAST.prev.prev)
            scale_rows(LAST)
            scatter_rows(LAST.prev)
            scatter_rows(LAST)
            pool.wait_ge(schedule_ready, 1)

            def store_tile(t):
                wait_apart(pool, (schedule_ready, 1), (expert_biased, t.n + 1))
                Q.dma_start(slot_out[bass.ds(t.n * TR, TR), :].rearrange("(p r) d -> p r d", r=RPT), tile_out[t.g][:, :, :]).then_inc(tile_stored[t.g], 16)

            tiles(store_tile, pool)
            for g in range(2):
                wait_dma(pool, tile_stored, Step(NT // 2 - 1, g))

            def fetch(st):
                used = [(combined, st.before.n + 1)] if st.before.exists else []
                wait_apart(pool, (schedule_ready, 1), (slots_cut, st.n + 1), *used)
                for j in range(TOP * G):
                    Q.indirect_dma_start(out=expert_rows[st.g][:, j, :], out_offset=None, in_=slot_out[:, :],
                                         in_offset=bass.IndirectOffsetOnAxis(ap=slot_idx[st.g][:, j:j + 1], axis=0)).then_inc(expert_rows_in[st.g], 16)

            token_steps(fetch, pool)


def kernel(x, L0_tok_pe, L0_attn_W_up, L0_attn_Wq, L0_attn_Wk, L0_attn_Wv, L0_attn_W_ig, L0_attn_b_ig, L0_attn_W_fg,
           L0_attn_b_fg, L0_attn_conv_w, L0_attn_conv_b, L0_attn_skip, L0_attn_W_down, L0_ffn_Wr, L0_ffn_br, L0_ffn_W1,
           L0_ffn_b1, L0_ffn_W2, L0_ffn_b2):
    import numpy as np
    from concourse import bacc
    from concourse.bass_utils import run_bass_kernel_spmd

    def turned(a):
        return np.ascontiguousarray(np.asarray(a).T)

    arrays = {
        "x": x, "pe": L0_tok_pe, "w_up": turned(L0_attn_W_up), "w_q": turned(L0_attn_Wq), "w_k": turned(L0_attn_Wk),
        "w_v": turned(L0_attn_Wv), "w_ig": turned(L0_attn_W_ig), "b_ig": L0_attn_b_ig, "w_fg": turned(L0_attn_W_fg),
        "b_fg": L0_attn_b_fg, "conv_w": L0_attn_conv_w, "conv_b": L0_attn_conv_b, "skip": L0_attn_skip,
        "w_down": turned(L0_attn_W_down), "w_r": turned(L0_ffn_Wr), "b_r": L0_ffn_br, "w1": L0_ffn_W1,
        "b1": turned(L0_ffn_b1), "w2": L0_ffn_W2, "b2": L0_ffn_b2,
    }
    arrays = {name: np.ascontiguousarray(a) for name, a in arrays.items()}
    nc = bacc.Bacc("TRN2", target_bir_lowering=False, num_devices=1)
    args = [nc.dram_tensor(name, a.shape, mybir.dt.from_np(a.dtype), kind="ExternalInput").ap() for name, a in arrays.items()]
    out = nc.dram_tensor("out", arrays["x"].shape + (arrays["pe"].shape[1],), F32, kind="ExternalOutput").ap()
    build(nc, *args, out)
    r = run_bass_kernel_spmd(nc, [arrays], core_ids=[0])
    return r.results[0]["out"]
```

```python
from contextlib import ExitStack

import concourse.bass as bass
from concourse import mybir

F32 = mybir.dt.float32
I32 = mybir.dt.int32
ALU = mybir.AluOpType
ACT = mybir.ActivationFunctionType

P = 128
LN_EPS = 1e-5
GATE_EPS = 1e-6
MASKED = -1e30


class Step:

    def __init__(self, chunk, group):
        self.c, self.g = chunk, group
        self.n = 2 * chunk + group
        self.exists = not (isinstance(chunk, int) and chunk < 0)

    @property
    def prev(self):
        return Step(self.c, 0) if self.g else Step(self.c - 1, 1)

    @property
    def next(self):
        return Step(self.c + 1, 0) if self.g else Step(self.c, 1)

    @property
    def before(self):
        return Step(self.c - 1, self.g)

    @property
    def after(self):
        return Step(self.c + 1, self.g)


def wait(engine, sem, per_step, step, i):
    if step.exists:
        engine.wait_ge(sem, per_step * step.n + i)


def wait_dma(engine, sems, step, dmas=1):
    if step.exists:
        engine.wait_ge(sems[step.g], 16 * dmas * (step.c + 1))


def wait_apart(engine, done, *waits):
    values = [v if isinstance(v, int) else engine.lower_val(v) for _, v in waits]
    engine.wait_ge(*done)
    for (sem, _), v in zip(waits, values):
        engine.wait_ge(sem, v)


def build(nc, x, pe, w_up, w_q, w_k, w_v, w_ig, b_ig, w_fg, b_fg, conv_w, conv_b, skip, w_down, w_r, b_r, w1, b1, w2, b2, out):
    B, S = x.shape
    VOCAB, D = pe.shape
    INNER = w_q.shape[0]
    NH = w_ig.shape[1]
    TAPS = conv_w.shape[1]
    DH = INNER // NH
    L = P
    NC = S // L
    G = B // 2
    KT = INNER // P
    HPK = NH // KT
    E1 = DH + 1
    GH = G * NH
    RW = L + 1
    VT = 10
    VR = VOCAB // VT
    PO = D + INNER
    GT = G * L
    assert VR * VT == VOCAB and KT == 2 and HPK == 4 and D == P and GT == 512 and NC * B == P

    NE, _, FH = w1.shape
    FK = FH // P
    TOP = 2
    TR = 4 * P
    RPT = TR // P
    REGION = B * S + TR
    NB = 2
    FIRST = 9 * NC // 16
    BT = TOP * B * L * FIRST // TR + NE
    NT = BT + TOP * B * L * (NC - FIRST) // TR + NE
    BE = NB * NE
    SLOT_ROWS = NE * REGION + TR
    NSTEP = 2 * NC
    TILE_SHIFT = TR.bit_length() - 1
    assert FK == 2 and BT % 2 == 0 and NT == BT + 4 * FIRST and TR == 1 << TILE_SHIFT and SLOT_ROWS < 1 << 24

    h1 = nc.dram_tensor("h1", (B, S, D), F32, kind="Internal").ap()
    slot_in = nc.dram_tensor("slot_in", (SLOT_ROWS, D), F32, kind="Internal").ap()
    slot_out = nc.dram_tensor("slot_out", (NT * TR, D), F32, kind="Internal").ap()
    table_x = nc.dram_tensor("table_x", (VOCAB, INNER), F32, kind="Internal").ap()
    table_po = nc.dram_tensor("table_po", (VOCAB, PO), F32, kind="Internal").ap()
    stab_dram = nc.dram_tensor("stab_dram", (2, GH * RW), F32, kind="Internal").ap()

    with ExitStack() as ctx:
        def sb(name, shape, dt=F32):
            return ctx.enter_context(nc.sbuf_tensor(name, shape, dt))

        def sem(name):
            return ctx.enter_context(nc.semaphore(name))

        def sem2(name):
            return [sem(f"{name}{g}") for g in range(2)]

        bank = [ctx.enter_context(nc.psum_tensor(f"bank{i}", [P, 512], F32)) for i in range(8)]
        SC, PJ, OX = bank[0:4], bank[4:6], bank[6:8]

        wr = sb("wr", [P, NE])
        brb = sb("brb", [P, NE])
        expert_i = sb("expert_i", [P, NE], I32)
        expert_f = sb("expert_f", [P, NE])
        region_i = sb("region_i", [P, NE], I32)
        region_f = sb("region_f", [P, NE])
        tile_i = sb("tile_i", [1, NT], I32)
        tile_f = sb("tile_f", [1, NT])
        earlier = sb("earlier", [P, P])
        ones_pp = sb("ones_pp", [P, P])
        zero_rows = sb("zero_rows", [P, D])
        b1_stage = sb("b1_stage", [P, FK, NE])
        tally_all = sb("tally_all", [P, NSTEP, NE])
        w1_all = sb("w1_all", [P, NE, FH + FK])
        w2_all = sb("w2_all", [P, NE, (FK + 1) * D])
        tally = sb("tally", [P, G, NE])
        slots_all = sb("slots_all", [P, NSTEP, TOP * G])
        out_slots = sb("out_slots", [P, NSTEP, TOP * G], I32)
        probs_all = sb("probs_all", [P, NSTEP, TOP * G])
        ident = sb("ident", [P, P])

        with ExitStack() as early_ctx:
            def early(name, shape, dt=F32):
                return early_ctx.enter_context(nc.sbuf_tensor(name, shape, dt))

            wup = early("wup", [P, 2 * INNER])
            pe_sb = early("pe_sb", [VR, VT, D])
            stats = early("stats", [VR, VT, 6])
            moments = early("moments", [VR, VT, 2])
            spread = early("spread", [VR, VT])
            rstd = early("rstd", [VR, VT])
            emb_n = early("emb_n", [VR, VT, D])
            emb_nT = early("emb_nT", [P, 2, VR])
            tx_sb = early("tx_sb", [VR, VT, INNER])
            tpo_sb = early("tpo_sb", [VR, VT, PO])
            ids_i = early("ids_i", [P, L], I32)
            ids_f = early("ids_f", [P, L])
        with ExitStack() as mixer_ctx:
            def mix(name, shape, dt=F32):
                return mixer_ctx.enter_context(nc.sbuf_tensor(name, shape, dt))

            decay = [mix(f"decay{g}", [P, GH, RW]) for g in range(2)]
            y = mix("y", [P, KT, GT])
            y_s = mix("y_s", [P, KT, GT])

            wq = mix("wq", [P, KT, INNER])
            wk = mix("wk", [P, KT, INNER])
            wvg = mix("wvg", [P, KT, INNER + 2 * NH])
            wd = mix("wd", [P, KT, D])
            taps = mix("taps", [P, KT, TAPS])
            convb = mix("convb", [P, KT])
            skipc = mix("skipc", [P, KT])
            gbias = mix("gbias", [P, G, 2, NH])
            ones_row = mix("ones_row", [GH, L])

            ids_T = mix("ids_T", [P, NC + 1, B], I32)

            x_idx = [mix(f"x_idx{g}", [P, G], I32) for g in range(2)]
            po_idx = [mix(f"po_idx{g}", [P, G], I32) for g in range(2)]
            x_rows = [mix(f"x_rows{g}", [P, G, INNER]) for g in range(2)]
            po_rows = [mix(f"po_rows{g}", [P, G, PO]) for g in range(2)]
            xup = [mix(f"xup{g}", [P, KT, G, TAPS - 1 + L]) for g in range(2)]
            conv = mix("conv", [P, KT, G, L])
            xm = [mix(f"xm{g}", [P, KT, GT]) for g in range(2)]
            qT = mix("qT", [P, KT, GT])
            kT = mix("kT", [P, KT, GT])
            k_tm = mix("k_tm", [P, G, INNER])
            v1 = [mix(f"v1{g}", [P, G, KT, HPK, HPK, E1]) for g in range(2)]
            v_w = mix("v_w", [P, GH, E1])
            gates = mix("gates", [P, G, 2, NH])
            gate_e = mix("gate_e", [P, G, 2, NH])
            gate_d = mix("gate_d", [P, G, 2, NH])
            gate_r = mix("gate_r", [P, G, 2, NH])
            gate_s = mix("gate_s", [P, G, 2, NH])
            gate_log = mix("gate_log", [P, 2, GH])
            rows_if = mix("rows_if", [GH, 2, L])
            row_b = mix("row_b", [GH, L])
            row_m = mix("row_m", [GH, L])
            m_carry = [mix(f"m_carry{g}", [GH, 1]) for g in range(2)]
            row_f = mix("row_f", [GH, 4, L])
            row_stab = mix("row_stab", [GH, RW])
            cols = [mix(f"cols{g}", [P, 4, GH]) for g in range(2)]
            state = [mix(f"state{g}", [P, G, NH, E1]) for g in range(2)]
            state_d = mix("state_d", [P, G, NH, E1])
            inter = mix("inter", [P, NH, E1])
            osum = mix("osum", [P, G, NH, E1])
            den = mix("den", [P, 4, GH])
            h_tm = mix("h_tm", [P, G, INNER])
            h1_sb = [mix(f"h1_sb{g}", [P, G, D]) for g in range(2)]
            ln_stats = mix("ln_stats", [P, G, 6])
            ln_mv = mix("ln_mv", [P, G, 2])
            ln_var = mix("ln_var", [P, G])
            minus_half = mix("minus_half", [P, G])
            ln_rstd = mix("ln_rstd", [P, G])
            xn = [mix(f"xn{g}", [P, G, D]) for g in range(2)]
            xnT = mix("xnT", [P, GT])
            logits = mix("logits", [P, G, NE])
            top_v = mix("top_v", [P, G, NE])
            top_i = mix("top_i", [P, G, NE], mybir.dt.uint32)
            top_f = mix("top_f", [P, TOP, G])
            onehot = mix("onehot", [P, TOP * G, NE])
            chosen = mix("chosen", [P, G, NE])
            below_top = mix("below_top", [P, G, NE])
            top_e = mix("top_e", [P, G, NE])
            top_sum = mix("top_sum", [P, G])
            top_r = mix("top_r", [P, G])
            place = mix("place", [P, G, NE])
            place_of = mix("place_of", [P, TOP * G, NE])
            slot_f = mix("slot_f", [P, TOP * G])
            slot_i = [mix(f"slot_i{g}", [P, TOP * G], I32) for g in range(2)]

        total = sb("total", [P, NB, NE])
        rows_from = sb("rows_from", [P, NB, NE])
        count = sb("count", [P, NB, NE])
        total_up = sb("total_up", [P, BE], I32)
        tiles_i = sb("tiles_i", [P, BE], I32)
        tiles_f = sb("tiles_f", [P, BE])
        tiles_end = sb("tiles_end", [P, BE])
        tile_from = sb("tile_from", [P, BE])
        unplaced = sb("unplaced", [P, NB, NE])
        shift = sb("shift", [P, NB, NE])
        shift_by = sb("shift_by", [P, NB, NE])
        row_by = sb("row_by", [1, BE])
        ones_e = sb("ones_e", [P, BE])
        pad_row = sb("pad_row", [1, NE], I32)
        tile_passed = sb("tile_passed", [1, NT])
        tile_shift = sb("tile_shift", [1, NT])
        tile_at = sb("tile_at", [1, NT])
        tile_row = sb("tile_row", [1, NT])
        wrapped = sb("wrapped", [1, NT])
        row_of = sb("row_of", [1, NT], I32)
        expert_of = sb("expert_of", [1, NT], I32)
        past = sb("past", [1, NT, BE])
        past_by = sb("past_by", [1, NT, BE])
        tile_rows = [sb(f"tile_rows{g}", [P, RPT, D]) for g in range(2)]
        slots_moved = sb("slots_moved", [P, NSTEP * TOP * G])
        beyond = sb("beyond", [P, NSTEP * TOP * G, NE])
        w1_now = [sb(f"w1_now{g}", [P, FH + FK]) for g in range(2)]
        w2_now = [sb(f"w2_now{g}", [P, FK + 1, D]) for g in range(2)]
        tile_xT = [sb(f"tile_xT{g}", [P, TR]) for g in range(2)]
        hidden = [sb(f"hidden{g}", [P, FK, TR]) for g in range(2)]
        tile_out = [sb(f"tile_out{g}", [P, RPT, D]) for g in range(2)]
        slot_idx = [sb(f"slot_idx{g}", [P, TOP * G], I32) for g in range(2)]
        expert_rows = [sb(f"expert_rows{g}", [P, TOP * G, D]) for g in range(2)]
        h1_again = [sb(f"h1_again{g}", [P, G, D]) for g in range(2)]
        mixed = sb("mixed", [P, G, D])
        out_rows = [sb(f"out_rows{g}", [P, G, D]) for g in range(2)]

        weights_in = sem("weights_in")
        pe_in = sem("pe_in")
        wup_in = sem("wup_in")
        ids_in = sem("ids_in")
        ident_zero = sem("ident_zero")
        ident_ready = sem("ident_ready")
        zeroed = sem("zeroed")
        moments_done = sem("moments_done")
        spread_done = sem("spread_done")
        rstd_done = sem("rstd_done")
        emb_ready = sem("emb_ready")
        emb_T = sem("emb_T")
        emb_T_kept = sem("emb_T_kept")
        up_done = sem("up_done")
        tx_kept = sem("tx_kept")
        tog_kept = sem("tog_kept")
        tpe_kept = sem("tpe_kept")
        table_out = sem("table_out")
        table_po_out = sem("table_po_out")
        ids_float = sem("ids_float")
        ids_turned = sem("ids_turned")
        ids_ready = sem("ids_ready")

        x_idx_cut = sem("x_idx_cut")
        po_idx_cut = sem("po_idx_cut")
        x_rows_in = sem2("x_rows_in")
        po_rows_in = sem2("po_rows_in")
        xup_T = sem("xup_T")
        xup_kept = sem("xup_kept")
        conv_taps = sem("conv_taps")
        carry_saved = sem("carry_saved")
        xm_ready = sem("xm_ready")
        qk_proj = sem("qk_proj")
        q_kept = sem("q_kept")
        k_kept = sem("k_kept")
        k_T = sem("k_T")
        k_tm_kept = sem("k_tm_kept")
        vg_proj = sem("vg_proj")
        v_kept = sem("v_kept")
        gates_biased = sem("gates_biased")
        gates_exp = sem("gates_exp")
        gates_sig = sem("gates_sig")
        gates_logged = sem("gates_logged")
        gates_T = sem("gates_T")
        row_steps = sem("row_steps")
        m_carried = sem("m_carried")
        row_factors = sem("row_factors")
        stab_out = sem2("stab_out")
        decay_in = sem2("decay_in")
        cols_T = sem("cols_T")
        cols_kept = sem("cols_kept")
        masked = sem("masked")
        v_weighted = sem("v_weighted")
        state_decayed = sem("state_decayed")
        weights_ready = sem("weights_ready")
        scores = sem("scores")
        sd_ready = sem("sd_ready")
        heads_out = sem("heads_out")
        inter_out = sem("inter_out")
        update_out = sem("update_out")
        inter_scaled = sem("inter_scaled")
        out_summed = sem("out_summed")
        state_kept = sem("state_kept")
        den_steps = sem("den_steps")
        h_normed = sem("h_normed")
        h_T = sem("h_T")
        og_T = sem("og_T")
        skip_mixed = sem("skip_mixed")
        y_ready = sem("y_ready")
        down_proj = sem("down_proj")
        h1_summed = sem("h1_summed")
        h1_stored = sem2("h1_stored")

        experts_iota = sem("experts_iota")
        consts_float = sem("consts_float")
        triangle_ready = sem("triangle_ready")
        empty_tiles_out = sem("empty_tiles_out")
        pad_rows_ready = sem("pad_rows_ready")
        pads_out = sem("pads_out")
        totals_out = sem("totals_out")
        sched_steps = sem("sched_steps")
        schedule_ready = sem("schedule_ready")
        ffn_weights_in = sem("ffn_weights_in")
        tile_rows_in = sem2("tile_rows_in")
        tile_T = sem("tile_T")
        tile_T_kept = sem("tile_T_kept")
        w1_picked = sem("w1_picked")
        w2_picked = sem("w2_picked")
        hidden_out = sem("hidden_out")
        gelu_done = sem("gelu_done")
        expert_out = sem("expert_out")
        expert_biased = sem("expert_biased")
        tile_stored = sem2("tile_stored")
        slots_cut = sem("slots_cut")
        h1_back = sem2("h1_back")
        expert_rows_in = sem2("expert_rows_in")
        first_added = sem("first_added")
        combined = sem("combined")
        out_stored = sem2("out_stored")
        ln_steps = sem("ln_steps")
        ln_scaled = sem("ln_scaled")
        xn_ready = sem("xn_ready")
        xn_T = sem("xn_T")
        xn_T_kept = sem("xn_T_kept")
        logits_out = sem("logits_out")
        top_steps = sem("top_steps")
        onehots = sem("onehots")
        onehot_ready = sem("onehot_ready")
        top_exp = sem("top_exp")
        tally_steps = sem("tally_steps")
        tallied = sem("tallied")
        prob_steps = sem("prob_steps")
        ranks_out = sem("ranks_out")
        place_steps = sem("place_steps")
        slots_ready = sem("slots_ready")
        scattered = sem2("scattered")

        block = ctx.enter_context(nc.Block())
        LAST = Step(NC - 1, 1)
        WEIGHTS_IN = 16 * (7 + 2 * KT + 2 * G + 2)

        def steps(slot, engine):
            for peeled in (Step(0, 0), Step(0, 1), Step(1, 0), Step(1, 1), Step(2, 0)):
                slot(peeled)
            with engine.Fori(2, NC - 1) as c:
                slot(Step(c, 1))
                slot(Step(c + 1, 0))
            slot(LAST)

        def own_blocks(v):
            whole = v[:, :, :, :, :, :]
            return bass.AP(whole.tensor, whole.offset, [whole.ap[0], [HPK * HPK * E1, G * KT], [(HPK + 1) * E1, HPK], [1, E1]])

        LAST_TILE = Step(NT // 2 - 1, 1)
        FFN_WEIGHTS_IN = 16 * (3 + FK)

        def is_last_tile(t):
            return t is LAST_TILE

        def tiles(slot, engine):
            for peeled in (Step(0, 0), Step(0, 1)):
                slot(peeled)
            with engine.Fori(1, NT // 2 - 1) as c:
                slot(Step(c, 0))
                slot(Step(c, 1))
            slot(LAST_TILE.prev)
            slot(LAST_TILE)


        def beside(pair, engine):
            pair(Step(BT // 2, 0), Step(BT // 2, 1), Step(0, 0))
            pair(Step(BT // 2 + 1, 0), Step(BT // 2 + 1, 1), Step(0, 1))
            with engine.Fori(1, FIRST - 1) as c:
                pair(Step(BT // 2 + 2 * c, 0), Step(BT // 2 + 2 * c, 1), Step(c, 0))
                pair(Step(BT // 2 + 2 * c + 1, 0), Step(BT // 2 + 2 * c + 1, 1), Step(c, 1))
            pair(Step(NT // 2 - 2, 0), Step(NT // 2 - 2, 1), Step(FIRST - 1, 0))
            pair(Step(NT // 2 - 1, 0), LAST_TILE, Step(FIRST - 1, 1))

        EARLY = 1
        LATE = 5

        def is_last(st):
            return st is LAST

        @block.sync
        def _(sp):
            sp.dma_start(pe_sb[:, :, :], pe.rearrange("(t p) d -> p t d", p=VR)).then_inc(pe_in, 16)
            sp.dma_start(wup[:, :], w_up).then_inc(wup_in, 16)
            sp.dma_start(ids_i[:, :], x.rearrange("b (c t) -> (b c) t", t=L)).then_inc(ids_in, 16)
            for dst, src in ((wq, w_q), (wk, w_k), (wd, w_down)):
                sp.dma_start(dst[:, :, :], src.rearrange("(k p) n -> p k n", p=P)).then_inc(weights_in, 16)
            for at, n, src in ((0, INNER, w_v), (INNER, NH, w_ig), (INNER + NH, NH, w_fg)):
                sp.dma_start(wvg[:, :, at:at + n], src.rearrange("(k p) n -> p k n", p=P)).then_inc(weights_in, 16)
            sp.dma_start(taps[:, :, :], conv_w.rearrange("(k p) t -> p k t", p=P)).then_inc(weights_in, 16)
            for dst, src in ((convb, conv_b), (skipc, skip)):
                for k in range(KT):
                    sp.dma_start(dst[:, k:k + 1], src[k * P:(k + 1) * P].rearrange("(p o) -> p o", o=1)).then_inc(weights_in, 16)
            for j, src in ((0, b_ig), (1, b_fg)):
                for b in range(G):
                    sp.dma_start(gbias[:, b, j, :], src.partition_broadcast(P)).then_inc(weights_in, 16)
            sp.dma_start(wr[:, :], w_r).then_inc(weights_in, 16)
            sp.dma_start(brb[:, :], b_r.partition_broadcast(P)).then_inc(weights_in, 16)
            sp.wait_ge(tx_kept, VT)
            sp.dma_start(table_x.rearrange("(t p) n -> p t n", p=VR), tx_sb[:, :, :]).then_inc(table_out, 16)
            sp.wait_ge(tog_kept, VT)
            sp.wait_ge(tpe_kept, 1)
            sp.dma_start(table_po.rearrange("(t p) n -> p t n", p=VR), tpo_sb[:, :, :]).then_inc(table_po_out, 16)

            def stabilisers(st):
                wait_apart(sp, (pe_in, 16), (row_factors, 4 * st.n + 4))
                wait_dma(sp, decay_in, st.before)
                sp.dma_start(stab_dram[st.g].rearrange("(r w) -> r w", w=RW), row_stab[:, :]).then_inc(stab_out[st.g], 16)
                wait_dma(sp, stab_out, st)
                wait(sp, heads_out, G, st.before, G)
                sp.dma_start(decay[st.g][:, :, :].rearrange("p r w -> p (r w)"), stab_dram[st.g].partition_broadcast(P)).then_inc(decay_in[st.g], 16)

            def store_h1(st):
                wait(sp, h1_summed, 1, st, 1)
                dst = h1[st.g * G:(st.g + 1) * G, bass.ds(st.c * L, L), :]
                sp.dma_start(dst.rearrange("b t d -> t b d"), h1_sb[st.g][:, :, :]).then_inc(h1_stored[st.g], 16)

            def slot(st):
                if st.prev.exists:
                    store_h1(st.prev)
                if not is_last(st):
                    stabilisers(st.next)

            stabilisers(Step(0, 0))
            sp.dma_start(w1_all[:, :, 0:FH], w1.rearrange("e p n -> p e n")).then_inc(ffn_weights_in, 16)
            sp.dma_start(b1_stage[:, :, :], b1.rearrange("(k p) e -> p k e", p=P)).then_inc(ffn_weights_in, 16)
            for k in range(FK):
                sp.dma_start(w2_all[:, :, k * D:(k + 1) * D], w2[:, k * P:(k + 1) * P, :].rearrange("e p n -> p e n")).then_inc(ffn_weights_in, 16)
            sp.dma_start(w2_all[:, :, FK * D:], b2.partition_broadcast(P)).then_inc(ffn_weights_in, 16)
            sp.wait_ge(zeroed, 1)
            sp.dma_start(slot_in[NE * REGION:SLOT_ROWS, :].rearrange("(r p) d -> p r d", p=P),
                         zero_rows[:, :].unsqueeze(1).broadcast_to([P, (SLOT_ROWS - NE * REGION) // P, D])).then_inc(empty_tiles_out, 16)
            steps(slot, sp)
            store_h1(LAST)
            for g in range(2):
                wait_dma(sp, h1_stored, Step(NC - 1, g))

            sp.wait_ge(pad_rows_ready, 1)
            for e in range(NE):
                row = sp.value_load(pad_row[0:1, e:e + 1], min_val=0, max_val=SLOT_ROWS - TR)
                sp.dma_start(slot_in[bass.ds(row, TR), :].rearrange("(p r) d -> p r d", r=RPT),
                             zero_rows[:, :].unsqueeze(1).broadcast_to([P, RPT, D])).then_inc(pads_out, 16)
            sp.wait_ge(schedule_ready, 1)
            sp.wait_ge(pads_out, 16 * NE)
            sp.wait_ge(empty_tiles_out, 16)
            for g in range(2):
                wait_dma(sp, scattered, Step(NC - 1, g), TOP * G)

            def load_tile(t):
                row = sp.value_load(row_of[0:1, bass.ds(t.n, 1)], min_val=0, max_val=SLOT_ROWS - TR)
                kept = [(tile_T, t.before.n + 1)] if t.before.exists else []
                wait_apart(sp, (schedule_ready, 1), *kept)
                sp.dma_start(tile_rows[t.g][:, :, :], slot_in[bass.ds(row, TR), :].rearrange("(p r) d -> p r d", r=RPT)).then_inc(tile_rows_in[t.g], 16)

            def load_h1(st):
                wait(sp, combined, 1, st.before, 1)
                src = h1[st.g * G:(st.g + 1) * G, bass.ds(st.c * L, L), :]
                sp.dma_start(h1_again[st.g][:, :, :], src.rearrange("b t d -> t b d")).then_inc(h1_back[st.g], 16)

            def store_out(st):
                wait(sp, combined, 1, st, 1)
                dst = out[st.g * G:(st.g + 1) * G, bass.ds(st.c * L, L), :]
                sp.dma_start(dst.rearrange("b t d -> t b d"), out_rows[st.g][:, :, :]).then_inc(out_stored[st.g], 16)

            def pair(t, t1, st):
                if not is_last_tile(t1):
                    load_tile(t.after)
                load_h1(st)
                if st.prev.exists and st.prev.prev.exists:
                    store_out(st.prev.prev)
                if not is_last_tile(t1):
                    load_tile(t1.after)

            load_tile(Step(0, 0))
            load_tile(Step(0, 1))
            with sp.Fori(1, BT // 2 + 1) as c:
                load_tile(Step(c, 0))
                load_tile(Step(c, 1))
            beside(pair, sp)
            store_out(Step(FIRST - 1, 0))
            store_out(Step(FIRST - 1, 1))
            load_h1(Step(FIRST, 0))
            load_h1(Step(FIRST, 1))
            with sp.Fori(FIRST + 1, NC) as c:
                store_out(Step(c - 1, 0))
                load_h1(Step(c, 0))
                store_out(Step(c - 1, 1))
                load_h1(Step(c, 1))
            store_out(LAST.prev)
            store_out(LAST)
            for g in range(2):
                wait_dma(sp, out_stored, Step(NC - 1, g))

        @block.tensor
        def _(pe_):
            T = nc.tensor
            pe_.wait_ge(ident_ready, 1)
            for t in range(VT + 1):
                if t < VT:
                    pe_.wait_ge(emb_ready, t + 1)
                    if t >= 2:
                        pe_.wait_ge(emb_T_kept, t - 1)
                    T.transpose(bank[t % 2][:, 0:VR], emb_n[:, t, :], ident[0:VR, 0:VR]).then_inc(emb_T, 1)
                if t == 0:
                    pe_.wait_ge(wup_in, 16)
                    continue
                pe_.wait_ge(emb_T_kept, t)
                if t >= 3:
                    pe_.wait_ge(tx_kept, t - 2)
                    pe_.wait_ge(tog_kept, t - 2)
                T.matmul(bank[2 + (t - 1) % 2][0:VR, :], emb_nT[:, (t - 1) % 2, :], wup[:, :], start=True, stop=True).then_inc(up_done, 1)
            pe_.wait_ge(ids_float, 1)
            T.transpose(bank[7][:, 0:P], ids_f[:, :], ident[:, :]).then_inc(ids_turned, 1)
            pe_.wait_ge(weights_in, WEIGHTS_IN)

            def turn_x(st):
                wait_dma(pe_, x_rows_in, st, G)
                for k in range(KT):
                    if k == 0:
                        wait(pe_, state_kept, G, st.before, 3)
                    else:
                        wait(pe_, row_steps, 5, st.prev, 1)
                        if st.prev.exists and st.prev.prev.exists and st.prev.prev.prev.exists:
                            wait(pe_, top_steps, 4, st.prev.prev.prev.prev, 1)
                    for b in range(G):
                        last = T.transpose(PJ[k][:, b * L:(b + 1) * L], x_rows[st.g][:, b, k * P:(k + 1) * P], ident[:, :])
                    last.then_inc(xup_T, 1)

            def project_qk(st, w, at):
                for m in range(KT):
                    if (at, m) == (0, 0):
                        wait(pe_, out_summed, G, st.prev, G)
                    elif (at, m) == (0, 1):
                        wait(pe_, inter_scaled, G, st.prev, G)
                    elif m == 0:
                        wait(pe_, state_kept, G, st.prev, G)
                    else:
                        wait(pe_, cols_kept, 1, st, 1)
                    for k in range(KT):
                        last = T.matmul(SC[at + m][:, :], w[:, k, m * P:(m + 1) * P], xm[st.g][:, k, :], start=k == 0, stop=k == KT - 1)
                    last.then_inc(qk_proj, 1)

            def turn_h(st):
                wait(pe_, h_normed, 1, st, 1)
                for k in range(KT):
                    for b in range(G):
                        last = T.transpose(OX[k][:, b * L:(b + 1) * L], h_tm[:, b, k * P:(k + 1) * P], ident[:, :])
                    last.then_inc(h_T, 1)

            def turn_og(st, tail):
                wait_dma(pe_, po_rows_in, st, G)
                for k in range(KT):
                    if not tail:
                        wait(pe_, q_kept, KT, st.next, k + 1)
                    for b in range(G):
                        last = T.transpose(SC[k][:, b * L:(b + 1) * L], po_rows[st.g][:, b, D + k * P:D + (k + 1) * P], ident[:, :])
                    last.then_inc(og_T, 1)

            def turn_k(st):
                wait(pe_, k_kept, KT, st, KT)
                for j in range(2):
                    if not is_last(st):
                        wait(pe_, xup_kept, KT, st.next, j + 1)
                    for b in (2 * j, 2 * j + 1):
                        for k in range(KT):
                            at = (b % 2) * INNER + k * P
                            last = T.transpose(PJ[j][:, at:at + P], kT[:, k, b * L:(b + 1) * L], ident[:, :])
                    last.then_inc(k_T, 1)

            def project_vg(st):
                wait(pe_, xm_ready, KT, st, KT)
                for b in range(G):
                    if b < 2:
                        if st.before.exists:
                            wait(pe_, skip_mixed, KT, st.before, b + 1)
                        else:
                            wait(pe_, v_kept, G, st.prev, G)
                            wait(pe_, gates_biased, G, st.prev, G)
                    else:
                        wait(pe_, gates_biased, G, st, b - 1)
                    for k in range(KT):
                        last = T.matmul(OX[b % 2][:, 0:INNER + 2 * NH], xm[st.g][:, k, b * L:(b + 1) * L], wvg[:, k, :], start=k == 0, stop=k == KT - 1)
                    last.then_inc(vg_proj, 1)

            def project_down(st, tail):
                wait(pe_, y_ready, KT, st, KT)
                if not tail:
                    wait(pe_, k_kept, KT, st.next, 1)
                for b in range(G):
                    for k in range(KT):
                        last = T.matmul(SC[2][:, b * D:(b + 1) * D], y[:, k, b * L:(b + 1) * L], wd[:, k, :], start=k == 0, stop=k == KT - 1)
                last.then_inc(down_proj, 1)

            def score(st, k, pairs=((0, 1), (2, 3))):
                if k == 0:
                    wait(pe_, q_kept, KT, st, KT)
                    wait(pe_, y_ready, KT, st.prev, KT)
                for pair in pairs:
                    if k == 0 and pair[0]:
                        wait(pe_, h1_summed, 1, st.prev, 1)
                    if k:
                        wait(pe_, sd_ready, NH, st, pair[1] + 1)
                    for b in range(G):
                        for r in pair:
                            rows = slice(r * DH, (r + 1) * DH)
                            one = T.matmul(SC[r][:, b * L:(b + 1) * L], kT[rows, k, b * L:(b + 1) * L], qT[rows, k, b * L:(b + 1) * L], start=True, stop=True)
                            if b == G - 1:
                                one.then_inc(scores, 1)

            def turn_gates(st):
                wait(pe_, gates_logged, 1, st, 1)
                wait(pe_, k_tm_kept, 2, st.prev, 2)
                ranked = st.prev.prev.prev if st.prev.exists and st.prev.prev.exists else st.prev
                if ranked.exists:
                    wait(pe_, place_steps, 4, ranked.prev, 1)
                for j in range(2):
                    last = T.transpose(PJ[1][0:GH, j * L:(j + 1) * L], gate_log[:, j, :], ident[:, :])
                last.then_inc(gates_T, 1)

            def turn_factors(st):
                wait_apart(pe_, (ident_ready, 1), (row_factors, 4 * st.n + 4))
                if st.prev.exists:
                    wait(pe_, sd_ready, NH, st.prev, NH)
                    if st.prev.prev.exists:
                        wait(pe_, xn_T_kept, 1, st.prev.prev.prev, 1)
                for j in range(4):
                    last = T.transpose(SC[3][:, j * GH:(j + 1) * GH], row_f[:, j, :], ident[0:GH, 0:GH])
                last.then_inc(cols_T, 1)

            def attend(st, b):
                o, i, u = (OX[0], OX[1], PJ[0]) if b % 2 == 0 else (SC[0], SC[1], SC[2])

                def own(k):
                    for r in range(HPK):
                        last = T.matmul(o[:, k * HPK * E1:(k + 1) * HPK * E1], decay[st.g][:, b * NH + k * HPK + r, 0:L],
                                        v1[st.g][:, b, k, r, :, :].rearrange("p q e -> p (q e)"), start=r == 0, stop=r == HPK - 1)
                    return last

                if b == 0:
                    wait(pe_, sd_ready, NH, st, HPK)
                    if not is_last(st):
                        wait(pe_, v_kept, G, st.next, G)
                        wait(pe_, gates_biased, G, st.next, G)
                if b >= 2:
                    wait(pe_, out_summed, G, st, b - 1)
                own(0)
                wait(pe_, state_kept, G, st.before, b + 1)
                for k in range(KT):
                    last = T.matmul(i[:, k * HPK * E1:(k + 1) * HPK * E1], qT[:, k, b * L:(b + 1) * L],
                                    state[st.g][:, b, k * HPK:(k + 1) * HPK, :].rearrange("p h e -> p (h e)"), start=True, stop=True)
                last.then_inc(inter_out, 1)
                if b == 0:
                    wait(pe_, k_tm_kept, 2, st, 2)
                    wait(pe_, v_weighted, 1, st, 1)
                if b >= 2:
                    wait(pe_, state_kept, G, st, b - 1)
                for k in range(KT):
                    at = b * NH + k * HPK
                    last = T.matmul(u[:, k * HPK * E1:(k + 1) * HPK * E1], k_tm[:, b, k * P:(k + 1) * P],
                                    v_w[:, at:at + HPK, :].rearrange("p h e -> p (h e)"), start=True, stop=True)
                last.then_inc(update_out, 1)
                if b == 0:
                    wait(pe_, sd_ready, NH, st, NH)
                own(1).then_inc(heads_out, 1)

            def turn_xn(st):
                wait(pe_, xn_ready, 1, st, 1)
                for b in range(G):
                    last = T.transpose(SC[3][:, b * L:(b + 1) * L], xn[st.g][:, b, :], ident[:, :])
                last.then_inc(xn_T, 1)

            def route(st):
                wait(pe_, xn_T_kept, 1, st, 1)
                if not (isinstance(st.c, int) and st.n >= 2 * NC - 3):
                    wait(pe_, row_steps, 5, st.next.next.next, 1)
                for b in range(G):
                    last = T.matmul(PJ[1][:, b * NE:(b + 1) * NE], xnT[:, b * L:(b + 1) * L], wr[:, :], start=True, stop=True)
                last.then_inc(logits_out, 1)

            def rank(st):
                wait(pe_, onehot_ready, 1, st, 1)
                if not (isinstance(st.c, int) and st.n >= 2 * NC - 3):
                    wait(pe_, k_tm_kept, 2, st.next.next.next, 2)
                T.matmul(PJ[1][:, 0:G * NE], earlier[:, :], chosen[:, :, :].rearrange("p b e -> p (b e)"), start=True, stop=False)
                T.matmul(PJ[1][:, 0:G * NE], ones_pp[:, :], tally[:, 0:G, :].rearrange("p b e -> p (b e)"), start=False, stop=True).then_inc(ranks_out, 1)

            def slot(st):
                nx, pv = st.next, st.prev
                pp = pv.prev if pv.exists else pv
                ppp = pp.prev if pp.exists else pp
                if not is_last(st):
                    turn_x(nx)
                wait(pe_, xm_ready, KT, st, KT)
                project_qk(st, wq, 0)
                if pv.exists:
                    turn_h(pv)
                project_qk(st, wk, 2)
                if pv.exists:
                    turn_og(pv, False)
                turn_k(st)
                if pv.exists:
                    project_down(pv, False)
                score(st, 0)
                if ppp.exists:
                    rank(ppp)
                if not is_last(st):
                    project_vg(nx)
                score(st, 1)
                attend(st, 0)
                if not is_last(st):
                    turn_gates(nx)
                if pp.exists:
                    turn_xn(pp)
                attend(st, 1)
                if pp.exists:
                    route(pp)
                attend(st, 2)
                if not is_last(st):
                    turn_factors(nx)
                attend(st, 3)

            pe_.wait_ge(zeroed, 2)
            pe_.wait_ge(triangle_ready, 2)
            pe_.wait_ge(consts_float, 1)
            pe_.wait_ge(tx_kept, VT)
            pe_.wait_ge(tog_kept, VT)
            pe_.wait_ge(ids_ready, 1)
            first = Step(0, 0)
            turn_x(first)
            project_vg(first)
            turn_gates(first)
            turn_factors(first)
            steps(slot, pe_)
            turn_h(LAST)
            turn_og(LAST, True)
            project_down(LAST, True)
            wait(pe_, top_steps, 4, LAST.prev.prev, 1)
            rank(LAST.prev.prev)
            turn_xn(LAST.prev)
            wait(pe_, place_steps, 4, LAST.prev.prev, 1)
            route(LAST.prev)
            wait(pe_, top_steps, 4, LAST.prev, 1)
            rank(LAST.prev)
            turn_xn(LAST)
            wait(pe_, place_steps, 4, LAST.prev, 1)
            route(LAST)
            wait(pe_, top_steps, 4, LAST, 1)
            rank(LAST)
            wait(pe_, place_steps, 4, LAST, 1)
            for half in range(NB):
                last = T.matmul(SC[3][:, half * NE:(half + 1) * NE], ones_pp[:, :], tally_all[:, (2 * FIRST if half == 0 else NSTEP) - 1, :], start=True, stop=True)
            last.then_inc(totals_out, 1)
            pe_.wait_ge(schedule_ready, 1)
            pe_.wait_ge(ffn_weights_in, FFN_WEIGHTS_IN)

            def turn_tile(t):
                wait_dma(pe_, tile_rows_in, t)
                wait(pe_, tile_T_kept, 1, t.prev, 1)
                for r in range(RPT):
                    last = T.transpose(bank[0][:, r * P:(r + 1) * P], tile_rows[t.g][:, r, :], ident[:, :])
                last.then_inc(tile_T, 1)

            def expand(t):
                wait(pe_, tile_T_kept, 1, t, 1)
                wait(pe_, w1_picked, 1, t, 1)
                for k in range(FK):
                    wait(pe_, gelu_done, FK, t.before, k + 1)
                    T.matmul(bank[2 + 2 * t.g + k][:, :], w1_now[t.g][:, k * P:(k + 1) * P], tile_xT[t.g][:, :], start=True, stop=True).then_inc(hidden_out, 1)

            def contract(t):
                wait(pe_, gelu_done, FK, t, FK)
                wait(pe_, w2_picked, 1, t, 1)
                wait(pe_, expert_biased, 1, t.before, 1)
                for r in range(RPT):
                    for k in range(FK):
                        last = T.matmul(bank[6 + t.g][:, r * P:(r + 1) * P], hidden[t.g][:, k, r * P:(r + 1) * P],
                                        w2_now[t.g][:, k, :], start=k == 0, stop=k == FK - 1)
                last.then_inc(expert_out, 1)

            def mlp(t):
                expand(t)
                if not is_last_tile(t):
                    turn_tile(t.next)
                if t.prev.exists:
                    contract(t.prev)

            turn_tile(Step(0, 0))
            tiles(mlp, pe_)
            contract(LAST_TILE)

        @block.vector
        def _(dve):
            V = nc.vector
            dve.wait_ge(pe_in, 16)
            for t in range(VT):
                last = V.bn_stats(stats[:, t, :], pe_sb[:, t, :])
            last.then_inc(moments_done, 1)
            dve.wait_ge(moments_done, 1)
            for t in range(VT):
                last = V.bn_aggr(moments[:, t, :], stats[:, t, :])
            last.then_inc(moments_done, 1)
            dve.wait_ge(moments_done, 2)
            V.tensor_scalar(spread[:, :], moments[:, :, 1], LN_EPS, None, ALU.add).then_inc(moments_done, 1)
            dve.wait_ge(spread_done, 1)
            V.reciprocal(rstd[:, :], spread[:, :]).then_inc(rstd_done, 1)
            dve.wait_ge(rstd_done, 1)
            for t in range(VT):
                V.tensor_scalar(emb_n[:, t, :], pe_sb[:, t, :], moments[:, t, 0:1], rstd[:, t:t + 1], ALU.subtract, ALU.mult).then_inc(emb_ready, 1)
            for t in range(VT + 1):
                if t < VT:
                    dve.wait_ge(emb_T, t + 1)
                    if t >= 2:
                        dve.wait_ge(up_done, t - 1)
                    V.tensor_copy(emb_nT[:, t % 2, :], bank[t % 2][:, 0:VR]).then_inc(emb_T_kept, 1)
                if t:
                    dve.wait_ge(up_done, t)
                    V.tensor_copy(tx_sb[:, t - 1, :], bank[2 + (t - 1) % 2][0:VR, 0:INNER]).then_inc(tx_kept, 1)
            dve.wait_ge(ids_in, 16)
            V.tensor_copy(ids_f[:, :], ids_i[:, :]).then_inc(ids_float, 1)
            dve.wait_ge(ids_turned, 1)
            V.tensor_copy(ids_T[:, 0:NC, :], bank[7][:, 0:P].rearrange("p (b c) -> p c b", c=NC)).then_inc(ids_ready, 1)
            dve.wait_ge(ids_ready, 1)

            def cut_x_idx(st):
                if st.before.exists:
                    wait_dma(dve, x_rows_in, st.before, G)
                V.tensor_copy(x_idx[st.g][:, :], ids_T[:, bass.ds(st.c, 1), st.g * G:(st.g + 1) * G].rearrange("p c b -> p (c b)")).then_inc(x_idx_cut, 1)

            def cut_po_idx(st):
                if st.before.exists:
                    wait_dma(dve, po_rows_in, st.before, G)
                V.tensor_copy(po_idx[st.g][:, :], ids_T[:, bass.ds(st.c, 1), st.g * G:(st.g + 1) * G].rearrange("p c b -> p (c b)")).then_inc(po_idx_cut, 1)

            def convolve(st):
                done = 0
                for k in range(KT):
                    for tap in range(TAPS - 2, -1, -1):
                        if tap == TAPS - 2:
                            wait(dve, xup_kept, KT, st, k + 1)
                        else:
                            wait(dve, conv_taps, KT * (TAPS - 1), st, done)
                        V.scalar_tensor_tensor(conv[:, k, :, :], xup[st.g][:, k, :, tap:tap + L], taps[:, k, tap:tap + 1],
                                               conv[:, k, :, :], ALU.mult, ALU.add).then_inc(conv_taps, 1)
                        done += 1
                wait(dve, conv_taps, KT * (TAPS - 1), st, KT * (TAPS - 1))
                V.tensor_copy(xup[st.g][:, :, :, 0:TAPS - 1].rearrange("p k b t -> p (k b) t"),
                              xup[st.g][:, :, :, L:L + TAPS - 1].rearrange("p k b t -> p (k b) t")).then_inc(carry_saved, 1)

            def gate_output(st):
                for k in range(KT):
                    wait(dve, h_T, KT, st, k + 1)
                    V.scalar_tensor_tensor(y_s[:, k, :], xm[st.g][:, k, :], skipc[:, k:k + 1], OX[k][:, :], ALU.mult, ALU.add).then_inc(skip_mixed, 1)
                for k in range(KT):
                    wait(dve, og_T, KT, st, k + 1)
                    wait(dve, skip_mixed, KT, st, k + 1)
                    wait(dve, down_proj, 1, st.prev, 1)
                    V.tensor_tensor(y[:, k, :], y_s[:, k, :], SC[k][:, :], ALU.mult).then_inc(y_ready, 1)

            def keep_k_tm(st):
                for j in range(2):
                    wait(dve, k_T, 2, st, j + 1)
                    wait(dve, update_out, G, st.prev, G)
                    V.tensor_copy(k_tm[:, 2 * j:2 * j + 2, :].rearrange("p b n -> p (b n)"), PJ[j][:, :]).then_inc(k_tm_kept, 1)

            def bias_gates(st, batches):
                for b in batches:
                    wait(dve, v_kept, G, st, b + 1)
                    if b == 0:
                        wait(dve, gates_exp, 1, st.prev, 1)
                    V.tensor_tensor(gates[:, b, :, :], OX[b % 2][:, INNER:INNER + 2 * NH].rearrange("p (j h) -> p j h", j=2), gbias[:, b, :, :], ALU.add).then_inc(gates_biased, 1)

            def add_residual(st):
                wait(dve, down_proj, 1, st, 1)
                wait_dma(dve, h1_stored, st.before)
                V.tensor_tensor(h1_sb[st.g][:, :, :], SC[2][:, :].rearrange("p (b d) -> p b d", b=G), po_rows[st.g][:, :, 0:D], ALU.add).then_inc(h1_summed, 1)

            def sigmoid_gates(st):
                wait(dve, gates_exp, 1, st, 1)
                V.tensor_scalar(gate_d[:, :, :, :], gate_e[:, :, :, :], 1.0, None, ALU.add).then_inc(gates_sig, 1)
                wait(dve, gates_sig, 3, st, 1)
                V.reciprocal(gate_r[:, :, :, :], gate_d[:, :, :, :]).then_inc(gates_sig, 1)
                wait(dve, gates_sig, 3, st, 2)
                wait(dve, gates_logged, 1, st.prev, 1)
                V.tensor_scalar(gate_s[:, :, :, :], gate_r[:, :, :, :], GATE_EPS, None, ALU.add).then_inc(gates_sig, 1)

            def weigh_scores(st, heads):
                for h in heads:
                    k, r = divmod(h, HPK)
                    wait(dve, weights_ready, NH, st, h + 1)
                    wait(dve, scores, NH, st, h + 1)
                    e = decay[st.g][:, :, 0:L].rearrange("p (b h) t -> p h b t", h=NH)[:, h]
                    V.tensor_tensor(e, SC[r][:, :].rearrange("p (b t) -> p b t", b=G), e, ALU.mult).then_inc(sd_ready, 1)

            def gate_rows(st):
                wait(dve, gates_T, 1, st, 1)
                V.tensor_copy(rows_if[:, :, :], PJ[1][0:GH, 0:2 * L].rearrange("p (j t) -> p j t", j=2)).then_inc(row_steps, 1)
                wait(dve, row_steps, 5, st, 1)
                V.tensor_tensor_scan(row_b[:, :], ones_row[:, :], rows_if[:, 1, :], 0.0, ALU.mult, ALU.add).then_inc(row_steps, 1)
                wait(dve, m_carried, 1, st.before, 1)
                wait(dve, row_factors, 4, st.prev, 4)
                V.tensor_tensor_scan(row_m[:, :], rows_if[:, 1, :], rows_if[:, 0, :], m_carry[st.g][:, 0:1], ALU.add, ALU.max).then_inc(row_steps, 1)
                wait(dve, row_steps, 5, st, 2)
                wait(dve, cols_T, 1, st.prev, 1)
                V.tensor_tensor(row_f[:, 0, :], rows_if[:, 0, :], row_b[:, :], ALU.subtract).then_inc(row_steps, 1)
                wait(dve, row_steps, 5, st, 3)
                wait_dma(dve, stab_out, st.prev)
                V.tensor_tensor(row_stab[:, 0:L], row_b[:, :], row_m[:, :], ALU.subtract).then_inc(row_steps, 1)

            def keep_factors(st):
                wait(dve, row_factors, 4, st, 4)
                V.tensor_copy(m_carry[st.g][:, :], row_m[:, L - 1:L]).then_inc(m_carried, 1)
                wait(dve, cols_T, 1, st, 1)
                wait(dve, v_weighted, 1, st.before, 1)
                V.tensor_copy(cols[st.g][:, :, :], SC[3][:, 0:4 * GH].rearrange("p (j r) -> p j r", j=4)).then_inc(cols_kept, 1)

            def sum_heads(st, b):
                o, i, u = (OX[0], OX[1], PJ[0]) if b % 2 == 0 else (SC[0], SC[1], SC[2])
                hs = slice(b * NH, (b + 1) * NH)
                wait(dve, inter_out, G, st, b + 1)
                if b:
                    wait(dve, out_summed, G, st, b)
                else:
                    wait(dve, h_normed, 1, st.prev, 1)
                V.tensor_tensor(inter[:, :, :], i[:, 0:NH * E1].rearrange("p (h e) -> p h e", h=NH),
                                cols[st.g][:, 1, hs].unsqueeze(2).broadcast_to([P, NH, E1]), ALU.mult).then_inc(inter_scaled, 1)
                wait(dve, inter_scaled, G, st, b + 1)
                wait(dve, heads_out, G, st, b + 1)
                V.tensor_tensor(osum[:, b, :, :], o[:, 0:NH * E1].rearrange("p (h e) -> p h e", h=NH), inter[:, :, :], ALU.add).then_inc(out_summed, 1)
                wait(dve, update_out, G, st, b + 1)
                wait(dve, state_decayed, 1, st, 1)
                uv = u[:, 0:NH * E1].rearrange("p (k r e) -> p r k e", k=KT, r=HPK)
                sv = state[st.g][:, b, :, :].rearrange("p (k r) e -> p r k e", k=KT)
                dv = state_d[:, b, :, :].rearrange("p (k r) e -> p r k e", k=KT)
                for r in range(HPK):
                    rows = slice(r * DH, (r + 1) * DH)
                    last = V.tensor_tensor(sv[rows, r], uv[rows, r], dv[rows, r], ALU.add)
                last.then_inc(state_kept, 1)

            def normalise(st):
                wait(dve, out_summed, G, st, G)
                dot = osum[:, :, :, DH].rearrange("p b h -> p (b h)")
                V.scalar_tensor_tensor(den[:, 0, :], dot, -1.0, dot, ALU.mult, ALU.max).then_inc(den_steps, 1)
                wait(dve, den_steps, 4, st, 1)
                V.tensor_tensor(den[:, 1, :], den[:, 0, :], cols[st.g][:, 2, :], ALU.max).then_inc(den_steps, 1)
                wait(dve, den_steps, 4, st, 2)
                V.tensor_scalar(den[:, 2, :], den[:, 1, :], GATE_EPS, None, ALU.add).then_inc(den_steps, 1)
                wait(dve, den_steps, 4, st, 3)
                V.reciprocal(den[:, 3, :], den[:, 2, :]).then_inc(den_steps, 1)
                wait(dve, den_steps, 4, st, 4)
                wait(dve, h_T, KT, st.prev, KT)
                V.tensor_tensor(h_tm[:, :, :].rearrange("p b (h e) -> p (b h) e", h=NH), osum[:, :, :, 0:DH].rearrange("p b h e -> p (b h) e"),
                                den[:, 3, :].unsqueeze(2).broadcast_to([P, GH, DH]), ALU.mult).then_inc(h_normed, 1)

            def row_moments(st):
                wait(dve, h1_summed, 1, st, 1)
                for b in range(G):
                    last = V.bn_stats(ln_stats[:, b, :], h1_sb[st.g][:, b, :])
                last.then_inc(ln_steps, 1)
                wait_apart(dve, (zeroed, 2), (ln_steps, 3 * st.n + 1))
                for b in range(G):
                    last = V.bn_aggr(ln_mv[:, b, :], ln_stats[:, b, :])
                last.then_inc(ln_steps, 1)
                wait(dve, ln_steps, 3, st, 2)
                V.tensor_scalar(ln_var[:, :], ln_mv[:, :, 1], LN_EPS, None, ALU.add).then_inc(ln_steps, 1)

            def normalise_rows(st):
                wait(dve, ln_scaled, 1, st, 1)
                wait_dma(dve, scattered, st.before, TOP * G)
                for b in range(G):
                    last = V.tensor_scalar(xn[st.g][:, b, :], h1_sb[st.g][:, b, :], ln_mv[:, b, 0:1], ln_rstd[:, b:b + 1], ALU.subtract, ALU.mult)
                last.then_inc(xn_ready, 1)

            def keep_logits(st):
                wait(dve, logits_out, 1, st, 1)
                V.tensor_tensor(logits[:, :, :], PJ[1][:, 0:G * NE].rearrange("p (b e) -> p b e", b=G), brb[:, :].unsqueeze(1).broadcast_to([P, G, NE]), ALU.add).then_inc(top_steps, 1)

            def find_top(st):
                kept = [(prob_steps, 3 * st.prev.n + 3)] if st.prev.exists else []
                wait_apart(dve, (zeroed, 2), (top_steps, 4 * st.n + 1), *kept)
                for b in range(G):
                    last = V.max(top_v[:, b, :], logits[:, b, :])
                last.then_inc(top_steps, 1)
                wait_apart(dve, (zeroed, 2), (top_steps, 4 * st.n + 2))
                for b in range(G):
                    last = V.max_index(top_i[:, b, :], top_v[:, b, :], logits[:, b, :])
                last.then_inc(top_steps, 1)
                V.tensor_tensor(below_top[:, :, :], top_v[:, :, :], top_v[:, :, 0:1].broadcast_to([P, G, NE]), ALU.subtract).then_inc(top_steps, 1)

            def choose(st):
                if st.prev.exists:
                    wait(dve, place_steps, 4, st.prev, 4)
                    wait(dve, tallied, 1, st.prev, 1)
                wait(dve, top_steps, 4, st, 3)
                V.tensor_copy(top_f[:, :, :], top_i[:, :, 0:TOP].rearrange("p b k -> p k b")).then_inc(onehots, 1)
                wait(dve, onehots, 3, st, 1)
                V.tensor_tensor(onehot[:, :, :], expert_f[:, :].unsqueeze(1).broadcast_to([P, TOP * G, NE]),
                                top_f[:, :, :].rearrange("p k b -> p (k b)").unsqueeze(2).broadcast_to([P, TOP * G, NE]), ALU.is_equal).then_inc(onehots, 1)
                wait(dve, onehots, 3, st, 2)
                V.tensor_tensor(chosen[:, :, :], onehot[:, 0:G, :], onehot[:, G:2 * G, :], ALU.add).then_inc(onehots, 1)
                wait(dve, onehots, 3, st, 3)
                for b in range(1, G):
                    one = V.tensor_tensor(tally[:, b, :], tally[:, b - 1, :], chosen[:, b - 1, :], ALU.add).then_inc(tally_steps, 1)
                    if b < G - 1:
                        wait(dve, tally_steps, G - 1, st, b)
                wait(dve, tally_steps, G - 1, st, G - 1)
                V.tensor_tensor(tally_all[:, bass.ds(st.n, 1), :].rearrange("p o e -> p (o e)"), tally[:, G - 1, :], chosen[:, G - 1, :], ALU.add).then_inc(onehot_ready, 1)

            def probabilities(st):
                wait(dve, top_exp, 1, st, 1)
                V.reduce_sum(top_sum[:, :], top_e[:, :, :], mybir.AxisListType.X).then_inc(prob_steps, 1)
                wait(dve, prob_steps, 3, st, 1)
                V.reciprocal(top_r[:, :], top_sum[:, :]).then_inc(prob_steps, 1)
                wait(dve, prob_steps, 3, st, 2)
                V.tensor_tensor(probs_all[:, bass.ds(st.n, 1), :].rearrange("p o (k b) -> p (o k) b", k=TOP), top_e[:, :, 0:TOP].rearrange("p b k -> p k b"),
                                top_r[:, :].unsqueeze(1).broadcast_to([P, TOP, G]), ALU.mult).then_inc(prob_steps, 1)

            def place_rows(st):
                wait(dve, ranks_out, 1, st, 1)
                V.tensor_tensor(place[:, :, :], PJ[1][:, 0:G * NE].rearrange("p (b e) -> p b e", b=G), region_f[:, :].unsqueeze(1).broadcast_to([P, G, NE]), ALU.add).then_inc(place_steps, 1)
                V.tensor_copy(tally[:, 0, :], tally_all[:, bass.ds(st.n, 1), :].rearrange("p o e -> p (o e)")).then_inc(tallied, 1)

            def place_tokens(st):
                wait(dve, place_steps, 4, st, 1)
                V.tensor_tensor(place_of[:, :, :].rearrange("p (k b) e -> p k (b e)", k=TOP), onehot[:, :, :].rearrange("p (k b) e -> p k (b e)", k=TOP),
                                place[:, :, :].rearrange("p b e -> p (b e)").unsqueeze(1).broadcast_to([P, TOP, G * NE]), ALU.mult).then_inc(place_steps, 1)
                wait(dve, place_steps, 4, st, 2)
                V.reduce_sum(slot_f[:, :], place_of[:, :, :], mybir.AxisListType.X).then_inc(place_steps, 1)
                wait(dve, place_steps, 4, st, 3)
                V.tensor_copy(slot_i[st.g][:, :], slot_f[:, :]).then_inc(slots_ready, 1)
                V.tensor_copy(slots_all[:, bass.ds(st.n, 1), :].rearrange("p o k -> p (o k)"), slot_f[:, :]).then_inc(place_steps, 1)

            def slot(st):
                nx, pv = st.next, st.prev
                pp = pv.prev if pv.exists else pv
                ppp = pp.prev if pp.exists else pp
                cut_po_idx(st)
                if not is_last(st):
                    cut_x_idx(st.after)
                if not is_last(st):
                    convolve(nx)
                if pv.exists:
                    gate_output(pv)
                if ppp.exists:
                    choose(ppp)
                keep_k_tm(st)
                if pv.exists:
                    add_residual(pv)
                weigh_scores(st, range(0, 4))
                if ppp.exists:
                    place_rows(ppp)
                if not is_last(st):
                    bias_gates(nx, range(G))
                    sigmoid_gates(nx)
                weigh_scores(st, range(4, 8))
                if pp.exists:
                    normalise_rows(pp)
                sum_heads(st, 0)
                if not is_last(st):
                    gate_rows(nx)
                if ppp.exists:
                    place_tokens(ppp)
                    probabilities(ppp)
                sum_heads(st, 1)
                if pv.exists:
                    row_moments(pv)
                if pp.exists:
                    keep_logits(pp)
                sum_heads(st, 2)
                if pp.exists:
                    find_top(pp)
                if not is_last(st):
                    keep_factors(nx)
                sum_heads(st, 3)
                normalise(st)

            first = Step(0, 0)
            cut_x_idx(first)
            cut_x_idx(first.next)
            V.memset(ones_row[:, :], 1.0)
            V.memset(ones_pp[:, :], 1.0)
            V.memset(zero_rows[:, :], 0.0)
            V.memset(tally[:, :, :], 0.0)
            V.memset(minus_half[:, :], -0.5)
            V.memset(ids_T[:, NC, :], 0)
            for g in range(2):
                V.memset(xup[g][:, :, :, 0:TAPS - 1], 0.0)
                V.memset(v1[g][:, :, :, :, :, :].rearrange("p b k r q e -> p (b k r q e)"), 0.0)
                V.memset(m_carry[g][:, :], 0.0)
                last = V.memset(state[g][:, :, :, :], 0.0)
            last.then_inc(zeroed, 1)
            dve.wait_ge(zeroed, 1)
            for g in range(2):
                last = V.memset(own_blocks(v1[g])[:, :, :, DH:E1], 1.0)
            last.then_inc(zeroed, 1)
            dve.wait_ge(zeroed, 2)
            dve.wait_ge(weights_in, WEIGHTS_IN)
            dve.wait_ge(experts_iota, 3)
            V.tensor_copy(expert_f[:, :], expert_i[:, :])
            V.tensor_copy(region_f[:, :], region_i[:, :])
            V.tensor_copy(tile_f[:, :], tile_i[:, :]).then_inc(consts_float, 1)
            dve.wait_ge(consts_float, 1)
            convolve(first)
            bias_gates(first, range(G))
            sigmoid_gates(first)
            gate_rows(first)
            keep_factors(first)
            steps(slot, dve)
            gate_output(LAST)
            add_residual(LAST)
            choose(LAST.prev.prev)
            place_rows(LAST.prev.prev)
            place_tokens(LAST.prev.prev)
            probabilities(LAST.prev.prev)
            normalise_rows(LAST.prev)
            row_moments(LAST)
            for st in (LAST.prev, LAST):
                keep_logits(st)
                find_top(st)
                choose(st)
                place_rows(st)
                place_tokens(st)
                probabilities(st)
                if st is not LAST:
                    normalise_rows(LAST)
            dve.wait_ge(totals_out, 1)
            V.memset(ones_e[:, :], 1.0)
            V.memset(rows_from[:, 0, :], 0.0)
            V.tensor_copy(total[:, :, :], SC[3][:, 0:BE].rearrange("p (b e) -> p b e", b=NB)).then_inc(sched_steps, 1)
            dve.wait_ge(sched_steps, 1)
            V.tensor_tensor(pad_row[:, :], total[0:1, NB - 1, :], region_f[0:1, :], ALU.add).then_inc(pad_rows_ready, 1)
            V.tensor_copy(rows_from[:, 1:NB, :], total[:, 0:NB - 1, :])
            V.tensor_copy(count[:, 0, :], total[:, 0, :])
            V.tensor_tensor(count[:, 1:NB, :], total[:, 1:NB, :], total[:, 0:NB - 1, :], ALU.subtract).then_inc(sched_steps, 1)
            dve.wait_ge(sched_steps, 2)
            V.tensor_scalar(total_up[:, :], count[:, :, :].rearrange("p b e -> p (b e)"), float(TR - 1), None, ALU.add).then_inc(sched_steps, 1)
            dve.wait_ge(sched_steps, 3)
            V.tensor_scalar(tiles_i[:, :], total_up[:, :], TILE_SHIFT, None, ALU.logical_shift_right).then_inc(sched_steps, 1)
            dve.wait_ge(sched_steps, 4)
            V.tensor_copy(tiles_f[:, :], tiles_i[:, :]).then_inc(sched_steps, 1)
            dve.wait_ge(sched_steps, 5)
            V.tensor_tensor_scan(tiles_end[:, :], ones_e[:, :], tiles_f[:, :], 0.0, ALU.mult, ALU.add).then_inc(sched_steps, 1)
            dve.wait_ge(sched_steps, 6)
            V.tensor_tensor(past[:, :, :], tile_f[:, :].unsqueeze(2).broadcast_to([1, NT, BE]), tiles_end[0:1, :].unsqueeze(1).broadcast_to([1, NT, BE]), ALU.is_ge)
            V.tensor_tensor(tile_from[:, :], tiles_end[:, :], tiles_f[:, :], ALU.subtract).then_inc(sched_steps, 1)
            dve.wait_ge(sched_steps, 7)
            V.scalar_tensor_tensor(unplaced[:, :, :], tile_from[:, :].rearrange("p (b e) -> p b e", b=NB), float(TR), rows_from[:, :, :], ALU.mult, ALU.subtract).then_inc(sched_steps, 1)
            dve.wait_ge(sched_steps, 8)
            V.tensor_tensor(shift[:, :, :], unplaced[:, :, :], region_f[:, :].unsqueeze(1).broadcast_to([P, NB, NE]), ALU.subtract).then_inc(sched_steps, 1)
            dve.wait_ge(sched_steps, 9)
            flat = shift[0:1, :, :].rearrange("p b e -> p (b e)")
            V.tensor_tensor(row_by[:, 0:BE - 1], flat[:, 1:BE], flat[:, 0:BE - 1], ALU.subtract)
            V.tensor_scalar(row_by[:, BE - 1:BE], flat[:, BE - 1:BE], -1.0, float(-NE * REGION), ALU.mult, ALU.add)
            V.tensor_copy(shift_by[:, :, 0:1], shift[:, :, 0:1])
            V.tensor_tensor(shift_by[:, :, 1:NE], shift[:, :, 1:NE], shift[:, :, 0:NE - 1], ALU.subtract).then_inc(sched_steps, 1)
            dve.wait_ge(sched_steps, 10)
            V.tensor_tensor(past_by[:, :, :], past[:, :, :], row_by[:, :].unsqueeze(1).broadcast_to([1, NT, BE]), ALU.mult)
            V.reduce_sum(tile_passed[:, :], past[:, :, :], mybir.AxisListType.X)
            V.tensor_scalar(tile_at[:, :], tile_f[:, :], float(TR), None, ALU.mult).then_inc(sched_steps, 1)
            dve.wait_ge(sched_steps, 11)
            V.reduce_sum(tile_shift[:, :], past_by[:, :, :], mybir.AxisListType.X)
            V.tensor_scalar(wrapped[:, :], tile_passed[:, :], float(NE), float(-NE), ALU.is_ge, ALU.mult).then_inc(sched_steps, 1)
            dve.wait_ge(sched_steps, 12)
            V.tensor_tensor(tile_row[:, :], tile_at[:, :], tile_shift[:, :], ALU.subtract)
            V.tensor_tensor(tile_passed[:, :], tile_passed[:, :], wrapped[:, :], ALU.add).then_inc(sched_steps, 1)
            dve.wait_ge(sched_steps, 13)
            V.tensor_scalar(expert_of[:, :], tile_passed[:, :], float(NE - 1), None, ALU.min)
            V.tensor_scalar(row_of[:, :], tile_row[:, :], float(NE * REGION), None, ALU.min).then_inc(schedule_ready, 1)
            dve.wait_ge(ffn_weights_in, FFN_WEIGHTS_IN)

            def keep_tile(t):
                wait(dve, tile_T, 1, t, 1)
                wait(dve, hidden_out, FK, t.before, FK)
                V.tensor_copy(tile_xT[t.g][:, :], bank[0][:, :]).then_inc(tile_T_kept, 1)

            def bias_expert(t):
                wait(dve, w2_picked, 1, t, 1)
                wait(dve, expert_out, 1, t, 1)
                wait_dma(dve, tile_stored, t.before)
                V.tensor_tensor(tile_out[t.g][:, :, :], bank[6 + t.g][:, :].rearrange("p (r d) -> p r d", r=RPT),
                                w2_now[t.g][:, FK:FK + 1, :].broadcast_to([P, RPT, D]), ALU.add).then_inc(expert_biased, 1)

            def mlp(t):
                if not is_last_tile(t):
                    keep_tile(t.next)
                if t.prev.exists:
                    bias_expert(t.prev)

            for k in range(FK):
                last = V.tensor_copy(w1_all[:, :, FH + k], b1_stage[:, k, :])
            last.then_inc(sched_steps, 1)
            dve.wait_ge(sched_steps, 14)
            slots = slots_all[:, :, :].rearrange("p s k -> p (s k)")
            wide = [P, NSTEP * TOP * G, NE]
            V.tensor_tensor(beyond[:, :, :], slots.unsqueeze(2).broadcast_to(wide), region_f[:, :].unsqueeze(1).broadcast_to(wide), ALU.is_ge).then_inc(sched_steps, 1)
            dve.wait_ge(sched_steps, 15)
            mid = 2 * FIRST * TOP * G
            for half, (lo, hi) in enumerate(((0, mid), (mid, wide[1]))):
                part = beyond[:, lo:hi, :]
                last = V.tensor_tensor(part, part, shift_by[:, half:half + 1, :].broadcast_to([P, hi - lo, NE]), ALU.mult)
            last.then_inc(sched_steps, 1)
            dve.wait_ge(sched_steps, 16)
            V.reduce_sum(slots_moved[:, :], beyond[:, :, :], mybir.AxisListType.X).then_inc(sched_steps, 1)
            dve.wait_ge(sched_steps, 17)
            V.tensor_tensor(out_slots[:, :, :].rearrange("p s k -> p (s k)"), slots_moved[:, :], slots, ALU.add).then_inc(sched_steps, 1)
            dve.wait_ge(sched_steps, 18)
            keep_tile(Step(0, 0))
            def cut_slots(st):
                if st.before.exists:
                    wait_dma(dve, expert_rows_in, st.before, TOP * G)
                V.tensor_copy(slot_idx[st.g][:, :], out_slots[:, bass.ds(st.n, 1), :].rearrange("p o k -> p (o k)")).then_inc(slots_cut, 1)

            def combine_first(st):
                wait_dma(dve, expert_rows_in, st, TOP * G)
                wait_dma(dve, h1_back, st)
                wait(dve, combined, 1, st.prev, 1)
                for b in range(G):
                    last = V.scalar_tensor_tensor(mixed[:, b, :], expert_rows[st.g][:, b, :], probs_all[:, bass.ds(st.n, 1), b], h1_again[st.g][:, b, :], ALU.mult, ALU.add)
                last.then_inc(first_added, 1)

            def combine_second(st):
                wait(dve, first_added, 1, st, 1)
                wait_dma(dve, out_stored, st.before)
                for b in range(G):
                    last = V.scalar_tensor_tensor(out_rows[st.g][:, b, :], expert_rows[st.g][:, G + b, :], probs_all[:, bass.ds(st.n, 1), G + b], mixed[:, b, :], ALU.mult, ALU.add)
                last.then_inc(combined, 1)

            def combine(st):
                combine_first(st)
                combine_second(st)

            def pair(t, t1, st):
                cut_slots(st)
                mlp(t)
                mlp(t1)
                if st.prev.exists:
                    combine(st.prev)

            mlp(Step(0, 0))
            mlp(Step(0, 1))
            with dve.Fori(1, BT // 2) as c:
                mlp(Step(c, 0))
                mlp(Step(c, 1))
            beside(pair, dve)
            bias_expert(LAST_TILE)
            combine(Step(FIRST - 1, 1))
            cut_slots(Step(FIRST, 0))
            with dve.Fori(FIRST, NC - 1) as c:
                cut_slots(Step(c, 1))
                combine(Step(c, 0))
                cut_slots(Step(c + 1, 0))
                combine(Step(c, 1))
            cut_slots(LAST)
            combine(LAST.prev)
            combine(LAST)

        @block.scalar
        def _(act):
            A = nc.scalar
            act.wait_ge(moments_done, 3)
            A.activation(spread[:, :], spread[:, :], ACT.Sqrt).then_inc(spread_done, 1)
            for t in range(VT):
                act.wait_ge(tx_kept, t + 1)
                A.activation(tpo_sb[:, t, D:PO], bank[2 + t % 2][0:VR, INNER:2 * INNER], ACT.Silu).then_inc(tog_kept, 1)
            act.wait_ge(weights_in, WEIGHTS_IN)
            act.wait_ge(zeroed, 2)

            def keep_x(st):
                for k in range(KT):
                    src = PJ[k][:, :].rearrange("p (b t) -> p b t", b=G)
                    wait(act, xup_T, KT, st, k + 1)
                    wait(act, carry_saved, 1, st.before, 1)
                    A.activation(xup[st.g][:, k, :, TAPS - 1:], src, ACT.Copy)
                    wait(act, xm_ready, KT, st.prev, k + 1)
                    A.activation(conv[:, k, :, :], src, ACT.Identity, bias=convb[:, k:k + 1], scale=taps[:, k, TAPS - 1:TAPS]).then_inc(xup_kept, 1)

            def keep_q(st):
                for m in range(KT):
                    wait(act, qk_proj, 2 * KT, st, m + 1)
                    wait(act, inter_out, G, st.prev, G)
                    A.activation(qT[:, m, :], SC[m][:, :], ACT.Copy, scale=float(DH) ** -0.5).then_inc(q_kept, 1)

            def keep_k(st):
                for m in range(KT):
                    wait(act, qk_proj, 2 * KT, st, KT + m + 1)
                    A.activation(kT[:, m, :], SC[2 + m][:, :], ACT.Copy).then_inc(k_kept, 1)

            def silu_x(st):
                for k in range(KT):
                    wait(act, conv_taps, KT * (TAPS - 1), st, (k + 1) * (TAPS - 1))
                    wait(act, skip_mixed, KT, st.before, k + 1)
                    A.activation(xm[st.g][:, k, :], conv[:, k, :, :].rearrange("p b t -> p (b t)"), ACT.Silu).then_inc(xm_ready, 1)

            def keep_v(st):
                for b in range(G):
                    wait(act, vg_proj, G, st, b + 1)
                    if b == 0:
                        wait(act, heads_out, G, st.before, G)
                        wait(act, v_weighted, 1, st.before, 1)
                    A.activation(own_blocks(v1[st.g])[:, KT * b:KT * (b + 1), :, 0:DH], OX[b % 2][:, 0:INNER].rearrange("p (k r e) -> p k r e", k=KT, r=HPK), ACT.Copy).then_inc(v_kept, 1)

            def exp_gates(st):
                wait(act, gates_biased, G, st, G)
                A.activation(gate_e[:, :, :, :].rearrange("p b j h -> p (b j h)"), gates[:, :, :, :].rearrange("p b j h -> p (b j h)"), ACT.Exp, scale=-1.0).then_inc(gates_exp, 1)

            def log_gates(st):
                wait(act, gates_sig, 3, st, 3)
                wait(act, gates_T, 1, st.prev, 1)
                A.activation(gate_log[:, :, :].rearrange("p j (b h) -> p j b h", b=G), gate_s[:, :, :, :].rearrange("p b j h -> p j b h"), ACT.Ln).then_inc(gates_logged, 1)

            def exp_weights(st, heads):
                for h in heads:
                    if h == 0:
                        wait(act, cols_kept, 1, st, 1)
                        wait(act, masked, 2, st, 2)
                    for b in range(G):
                        e = decay[st.g][:, b * NH + h, 0:L]
                        last = A.activation(e, e, ACT.Exp, bias=cols[st.g][:, 0, b * NH + h:b * NH + h + 1])
                    last.then_inc(weights_ready, 1)

            def exp_rows(st):
                wait(act, row_steps, 5, st, 5)
                wait(act, cols_T, 1, st.prev, 1)
                A.activation(row_f[:, 1, :], row_stab[:, 0:L], ACT.Exp, bias=m_carry[st.g][:, 0:1]).then_inc(row_factors, 1)
                A.activation(row_stab[:, L:RW], row_stab[:, L - 1:L], ACT.Exp, bias=m_carry[st.g][:, 0:1]).then_inc(row_factors, 1)
                A.activation(row_f[:, 2, :], row_m[:, :], ACT.Exp, scale=-1.0).then_inc(row_factors, 1)
                A.activation(row_f[:, 3, :], row_f[:, 0, :], ACT.Exp, bias=row_stab[:, L - 1:L]).then_inc(row_factors, 1)

            def keep_xn(st):
                wait(act, xn_T, 1, st, 1)
                wait(act, logits_out, 1, st.prev, 1)
                A.activation(xnT[:, :], SC[3][:, :], ACT.Copy).then_inc(xn_T_kept, 1)

            def exp_top(st):
                wait(act, top_steps, 4, st, 4)
                wait(act, prob_steps, 3, st.prev, 3)
                A.activation(top_e[:, :, :].rearrange("p b e -> p (b e)"), below_top[:, :, :].rearrange("p b e -> p (b e)"), ACT.Exp).then_inc(top_exp, 1)

            def slot(st):
                nx, pv = st.next, st.prev
                pp = pv.prev if pv.exists else pv
                ppp = pp.prev if pp.exists else pp
                if not is_last(st):
                    keep_x(nx)
                keep_q(st)
                started = st.n if isinstance(st.n, int) else 1
                if started:
                    exp_weights(st, range(0, EARLY))
                keep_k(st)
                if not is_last(st):
                    silu_x(nx)
                exp_weights(st, range(EARLY if started else 0, LATE))
                if not is_last(st):
                    keep_v(nx)
                    exp_gates(nx)
                if ppp.exists:
                    exp_top(ppp)
                exp_weights(st, range(LATE, NH))
                if not is_last(st):
                    log_gates(nx)
                if pp.exists:
                    keep_xn(pp)
                if not is_last(st):
                    exp_rows(nx)

            first = Step(0, 0)
            keep_x(first)
            silu_x(first)
            keep_v(first)
            exp_gates(first)
            log_gates(first)
            exp_rows(first)
            steps(slot, act)
            exp_top(LAST.prev.prev)
            for st in (LAST.prev, LAST):
                keep_xn(st)
                exp_top(st)
            act.wait_ge(schedule_ready, 1)
            act.wait_ge(ffn_weights_in, FFN_WEIGHTS_IN)

            def bend(t):
                wait(act, w1_picked, 1, t, 1)
                for k in range(FK):
                    wait(act, hidden_out, FK, t, k + 1)
                    if k == 0:
                        wait(act, expert_out, 1, t.before, 1)
                    A.activation(hidden[t.g][:, k, :], bank[2 + 2 * t.g + k][:, :], ACT.Gelu,
                                 bias=w1_now[t.g][:, FH + k:FH + k + 1]).then_inc(gelu_done, 1)

            def store_tile(t):
                wait(act, expert_biased, 1, t, 1)
                act.dma_start(slot_out[bass.ds(t.n * TR, TR), :].rearrange("(p r) d -> p r d", r=RPT), tile_out[t.g][:, :, :]).then_inc(tile_stored[t.g], 16)

            def expert_number(t):
                return act.value_load(expert_of[0:1, bass.ds(t.n, 1)], min_val=0, max_val=NE - 1)

            def pick_w1(t, e):
                used = [(hidden_out, FK * t.before.n + FK), (gelu_done, FK * t.before.n + FK)] if t.before.exists else []
                wait_apart(act, (schedule_ready, 1), *used)
                A.activation(w1_now[t.g][:, :], w1_all[:, bass.ds(e, 1), :].rearrange("p o n -> p (o n)"), ACT.Copy).then_inc(w1_picked, 1)

            def pick_w2(t, e):
                used = [(expert_biased, t.before.n + 1)] if t.before.exists else []
                wait_apart(act, (schedule_ready, 1), *used)
                A.activation(w2_now[t.g][:, :, :].rearrange("p k n -> p (k n)"), w2_all[:, bass.ds(e, 1), :].rearrange("p o n -> p (o n)"), ACT.Copy).then_inc(w2_picked, 1)

            def mlp(t):
                if not is_last_tile(t):
                    e = expert_number(t.next)
                    pick_w1(t.next, e)
                bend(t)
                if t.prev.exists:
                    store_tile(t.prev)
                if not is_last_tile(t):
                    pick_w2(t.next, e)

            act.wait_ge(sched_steps, 14)
            e = expert_number(Step(0, 0))
            pick_w1(Step(0, 0), e)
            pick_w2(Step(0, 0), e)
            tiles(mlp, act)
            store_tile(LAST_TILE)

        @block.gpsimd
        def _(pool):
            Q = nc.gpsimd
            Q.memset(ident[:, :], 0.0).then_inc(ident_zero, 1)
            pool.wait_ge(ident_zero, 1)
            Q.affine_select(out=ident[:, :], in_=ident[:, :], compare_op=ALU.not_equal, fill=1.0, base=0,
                            pattern=[[-1, P]], channel_multiplier=1).then_inc(ident_ready, 1)
            Q.iota(expert_i[:, :], pattern=[[1, NE]], base=0, channel_multiplier=0).then_inc(experts_iota, 1)
            Q.iota(region_i[:, :], pattern=[[REGION, NE]], base=0, channel_multiplier=0).then_inc(experts_iota, 1)
            Q.iota(tile_i[:, :], pattern=[[1, NT]], base=0, channel_multiplier=0).then_inc(experts_iota, 1)
            Q.memset(earlier[:, :], 1.0).then_inc(triangle_ready, 1)
            pool.wait_ge(triangle_ready, 1)
            Q.affine_select(out=earlier[:, :], in_=earlier[:, :], compare_op=ALU.is_gt, fill=0.0, base=0,
                            pattern=[[1, P]], channel_multiplier=-1).then_inc(triangle_ready, 1)
            pool.wait_ge(pe_in, 16)
            Q.tensor_copy(tpo_sb[:, :, 0:D], pe_sb[:, :, :]).then_inc(tpe_kept, 1)
            pool.wait_ge(table_out, 16)

            def gather(rows, table, idx, sems, st):
                for b in range(G):
                    Q.indirect_dma_start(out=rows[st.g][:, b, :], out_offset=None, in_=table[:, :],
                                         in_offset=bass.IndirectOffsetOnAxis(ap=idx[st.g][:, b:b + 1], axis=0)).then_inc(sems[st.g], 16)

            def gather_x(st):
                kept = [(xup_T, KT * st.before.n + KT)] if st.before.exists else []
                wait_apart(pool, (table_out, 16), (x_idx_cut, st.n + 1), *kept)
                gather(x_rows, table_x, x_idx, x_rows_in, st)

            def gather_po(st):
                kept = [(h1_summed, st.before.n + 1)] if st.before.exists else []
                wait_apart(pool, (table_po_out, 16), (po_idx_cut, st.n + 1), *kept)
                gather(po_rows, table_po, po_idx, po_rows_in, st)

            def mask(st):
                wait_apart(pool, (ident_ready, 1), (decay_in[st.g], 16 * (st.c + 1)))
                for j in range(2):
                    m = decay[st.g][:, j * GH // 2:(j + 1) * GH // 2, 0:L]
                    Q.affine_select(out=m, in_=m, compare_op=ALU.is_ge, fill=MASKED, base=0,
                                    pattern=[[0, GH // 2], [1, L]], channel_multiplier=-1).then_inc(masked, 1)

            def scale_rows(st):
                wait(pool, ln_steps, 3, st, 3)
                wait(pool, xn_ready, 1, st.prev, 1)
                Q.tensor_tensor(ln_rstd[:, :], ln_var[:, :], minus_half[:, :], ALU.pow).then_inc(ln_scaled, 1)

            def scatter_rows(st):
                wait_apart(pool, (triangle_ready, 2), (slots_ready, st.n + 1))
                for j in range(TOP * G):
                    Q.indirect_dma_start(out=slot_in[:, :], out_offset=bass.IndirectOffsetOnAxis(ap=slot_i[st.g][:, j:j + 1], axis=0),
                                         in_=xn[st.g][:, j % G, :], in_offset=None).then_inc(scattered[st.g], 16)

            def slot(st):
                pp = st.prev.prev if st.prev.exists else st.prev
                ppp = pp.prev if pp.exists else pp
                wait(pool, cols_kept, 1, st, 1)
                wait(pool, v_kept, G, st, G)
                wait(pool, update_out, G, st.prev, G)
                Q.tensor_tensor(v_w[:, :, :].rearrange("p (m r) e -> p m r e", r=HPK), own_blocks(v1[st.g]),
                                cols[st.g][:, 3, :].rearrange("p (m r) -> p m r", r=HPK).unsqueeze(3).broadcast_to([P, G * KT, HPK, E1]), ALU.mult).then_inc(v_weighted, 1)
                wait(pool, state_kept, G, st.prev, G)
                Q.tensor_tensor(state_d[:, :, :, :].rearrange("p b h e -> p (b h) e"), state[st.g][:, :, :, :].rearrange("p b h e -> p (b h) e"),
                                decay[st.g][:, :, L:RW].broadcast_to([P, GH, E1]), ALU.mult).then_inc(state_decayed, 1)
                gather_po(st)
                if ppp.exists and ppp.prev.exists:
                    scatter_rows(ppp.prev)
                if pp.exists:
                    scale_rows(pp)
                if not is_last(st):
                    gather_x(st.after)
                    mask(st.next)
                else:
                    scatter_rows(ppp)

            first = Step(0, 0)
            gather_x(first)
            gather_x(first.next)
            mask(first)
            steps(slot, pool)
            scale_rows(LAST.prev)
            scatter_rows(LAST.prev.prev)
            scale_rows(LAST)
            scatter_rows(LAST.prev)
            scatter_rows(LAST)
            pool.wait_ge(schedule_ready, 1)

            for g in range(2):
                wait_dma(pool, tile_stored, Step(BT // 2 - 1, g))

            def fetch(st, rows):
                used = [(combined, st.before.n + 1)] if st.before.exists else []
                wait_apart(pool, (schedule_ready, 1), (slots_cut, st.n + 1), *used)
                for j in range(TOP * G):
                    Q.indirect_dma_start(out=expert_rows[st.g][:, j, :], out_offset=None, in_=slot_out[0:rows, :],
                                         in_offset=bass.IndirectOffsetOnAxis(ap=slot_idx[st.g][:, j:j + 1], axis=0)).then_inc(expert_rows_in[st.g], 16)

            fetch(Step(0, 0), BT * TR)
            fetch(Step(0, 1), BT * TR)
            with pool.Fori(1, FIRST) as c:
                fetch(Step(c, 0), BT * TR)
                fetch(Step(c, 1), BT * TR)
            for g in range(2):
                wait_dma(pool, tile_stored, Step(NT // 2 - 1, g))
            with pool.Fori(FIRST, NC) as c:
                fetch(Step(c, 0), NT * TR)
                fetch(Step(c, 1), NT * TR)


def kernel(x, L0_tok_pe, L0_attn_W_up, L0_attn_Wq, L0_attn_Wk, L0_attn_Wv, L0_attn_W_ig, L0_attn_b_ig, L0_attn_W_fg,
           L0_attn_b_fg, L0_attn_conv_w, L0_attn_conv_b, L0_attn_skip, L0_attn_W_down, L0_ffn_Wr, L0_ffn_br, L0_ffn_W1,
           L0_ffn_b1, L0_ffn_W2, L0_ffn_b2):
    import numpy as np
    from concourse import bacc
    from concourse.bass_utils import run_bass_kernel_spmd

    def turned(a):
        return np.ascontiguousarray(np.asarray(a).T)

    arrays = {
        "x": x, "pe": L0_tok_pe, "w_up": turned(L0_attn_W_up), "w_q": turned(L0_attn_Wq), "w_k": turned(L0_attn_Wk),
        "w_v": turned(L0_attn_Wv), "w_ig": turned(L0_attn_W_ig), "b_ig": L0_attn_b_ig, "w_fg": turned(L0_attn_W_fg),
        "b_fg": L0_attn_b_fg, "conv_w": L0_attn_conv_w, "conv_b": L0_attn_conv_b, "skip": L0_attn_skip,
        "w_down": turned(L0_attn_W_down), "w_r": turned(L0_ffn_Wr), "b_r": L0_ffn_br, "w1": L0_ffn_W1,
        "b1": turned(L0_ffn_b1), "w2": L0_ffn_W2, "b2": L0_ffn_b2,
    }
    arrays = {name: np.ascontiguousarray(a) for name, a in arrays.items()}
    nc = bacc.Bacc("TRN2", target_bir_lowering=False, num_devices=1)
    args = [nc.dram_tensor(name, a.shape, mybir.dt.from_np(a.dtype), kind="ExternalInput").ap() for name, a in arrays.items()]
    out = nc.dram_tensor("out", arrays["x"].shape + (arrays["pe"].shape[1],), F32, kind="ExternalOutput").ap()
    build(nc, *args, out)
    r = run_bass_kernel_spmd(nc, [arrays], core_ids=[0])
    return r.results[0]["out"]
```
